# Optimizing a Trainium2 kernel written in Bass

```python
import numpy as np
import jax
import jax.numpy as jnp

def _softmax(x, axis=-1):
    return jax.nn.softmax(x, axis=axis)

def _gelu(x):
    return jax.nn.gelu(x, approximate=True)

def _silu(x):
    return jax.nn.silu(x)

def _sigmoid(x):
    return jax.nn.sigmoid(x)

def _layernorm(x, axis=-1, eps=1e-05):
    m = jnp.mean(x, axis=axis, keepdims=True)
    v = jnp.var(x, axis=axis, keepdims=True)
    return (x - m) / jnp.sqrt(v + eps)

def _scatter_add(tgt, idx, src, axis=0):
    return tgt.at[idx].add(src)

def _segment_sum(src, seg, n):
    return jax.ops.segment_sum(src, seg, n)
kernel_name = 'mk_gnn_resnorm_d2_gnn_r8_c9614d'

def setup_inputs(seed: int=0):
    np.random.seed(seed)
    _w = jnp.asarray

    def _rec_inputs():
        import jax
        import jax.numpy as jnp
        _gk = jax.random.key(seed)
        x = -0.000202 + 1 * jax.random.normal(jax.random.fold_in(_gk, 1), (12500, 64), jnp.float32)
        src = jax.random.randint(jax.random.fold_in(_gk, 2), (200000,), 0, 12500, jnp.int32)
        dst = jax.random.randint(jax.random.fold_in(_gk, 3), (200000,), 0, 12500, jnp.int32)
        _o = jnp.argsort(dst, stable=True)
        src = src[_o]
        dst = dst[_o]
        edge_attr_32 = 0.000155561 + 1.00019 * jax.random.normal(jax.random.fold_in(_gk, 12), (200000, 32), jnp.float32)
        edge_weight = jax.random.uniform(jax.random.fold_in(_gk, 14), (200000,), jnp.float32, 0.0, 0.999999)
        edge_weight_n2 = jax.random.uniform(jax.random.fold_in(_gk, 15), (200000,), jnp.float32, 0.0, 0.999999)
        return (x, src, dst, edge_attr_32, edge_weight, edge_weight_n2)
    x, src, dst, edge_attr_32, edge_weight, edge_weight_n2 = _rec_inputs()

    def _L0_gnn_setup():
        import jax, jax.numpy as jnp
        import numpy as np
        N = 12500
        E = 150000
        F = 64
        D = 32
        G = 64
        EPS = 1e-05
        NEG_SLOPE = 0.01

        def _cgconv(x, src, dst, attr, Wf, bf, Ws, bs):
            z = jnp.concatenate([x[dst], x[src], attr], axis=-1)
            m = jax.nn.sigmoid(z @ Wf + bf) * jax.nn.softplus(z @ Ws + bs)
            agg = jax.ops.segment_sum(m, dst, num_segments=N)
            return agg + x

        def _graph_norm(x, batch, w, b, ms):
            cnt = jax.ops.segment_sum(jnp.ones((N,), x.dtype), batch, num_segments=G)
            cnt = jnp.maximum(cnt, 1.0)[:, None]
            mean = jax.ops.segment_sum(x, batch, num_segments=G) / cnt
            out = x - mean[batch] * ms
            var = jax.ops.segment_sum(out * out, batch, num_segments=G) / cnt
            std = jnp.sqrt(var + EPS)
            return w * out / std[batch] + b

        def _leaky_relu(x):
            return jnp.where(x >= 0, x, NEG_SLOPE * x)
        key = jax.random.key(seed)
        ks = jax.random.split(key, 16)
        Z = 2 * F + D
        s = 1.0 / np.sqrt(Z)
        inp = {'x': jax.random.normal(ks[0], (N, F), dtype=jnp.float32), 'index': jax.random.randint(ks[1], (2, E), 0, N, dtype=jnp.int64), 'attr': jax.random.normal(ks[2], (E, D), dtype=jnp.float32), 'batch': jnp.sort(jax.random.randint(ks[3], (N,), 0, G, dtype=jnp.int64)), 'Wf1': jax.random.uniform(ks[4], (Z, F), jnp.float32, -s, s), 'bf1': jax.random.uniform(ks[5], (F,), jnp.float32, -s, s), 'Ws1': jax.random.uniform(ks[6], (Z, F), jnp.float32, -s, s), 'bs1': jax.random.uniform(ks[7], (F,), jnp.float32, -s, s), 'gw1': jnp.ones((F,), jnp.float32), 'gb1': jnp.zeros((F,), jnp.float32), 'gm1': jnp.ones((F,), jnp.float32), 'Wf2': jax.random.uniform(ks[8], (Z, F), jnp.float32, -s, s), 'bf2': jax.random.uniform(ks[9], (F,), jnp.float32, -s, s), 'Ws2': jax.random.uniform(ks[10], (Z, F), jnp.float32, -s, s), 'bs2': jax.random.uniform(ks[11], (F,), jnp.float32, -s, s), 'gw2': jnp.ones((F,), jnp.float32), 'gb2': jnp.zeros((F,), jnp.float32), 'gm2': jnp.ones((F,), jnp.float32)}
        return inp
    _L0_gnn_all = _L0_gnn_setup()
    _L0_gnn_in = {k: v for k, v in _L0_gnn_all.items() if k in ('Wf1', 'bf1', 'Ws1', 'bs1', 'gw1', 'gb1', 'gm1', 'Wf2', 'bf2', 'Ws2', 'bs2', 'gw2', 'gb2', 'gm2')}
    del _L0_gnn_all

    def _L1_gnn_setup():
        import jax, jax.numpy as jnp
        import numpy as np
        N, E, D_IN, D_OUT = (8192, 131072, 64, 64)
        EPS = 1e-08
        key = jax.random.key(seed)
        ks = jax.random.split(key, 8)
        h = jax.random.normal(ks[0], (N, D_IN), dtype=jnp.float32)
        edge_index = jax.random.randint(ks[1], (2, E), 0, N, dtype=jnp.int64 if jax.config.jax_enable_x64 else jnp.int32)
        adj_v = jax.random.uniform(ks[2], (E,), dtype=jnp.float32)
        deg_v = jax.random.uniform(ks[3], (E,), dtype=jnp.float32)
        W = jax.random.normal(ks[4], (D_IN, D_OUT), dtype=jnp.float32) / np.sqrt(D_IN)
        b = jax.random.normal(ks[5], (D_OUT,), dtype=jnp.float32) * 0.01
        deg_coeff = jnp.array([0.5, 0.0], dtype=jnp.float32)
        coeff_param = jnp.zeros((3,), dtype=jnp.float32)
        scale_param = 2.0 * jnp.ones((1,), dtype=jnp.float32)
        return {'h': h, 'edge_index': edge_index, 'adj_v': adj_v, 'deg_v': deg_v, 'W': W, 'b': b, 'deg_coeff': deg_coeff, 'coeff_param': coeff_param, 'scale_param': scale_param}
    _L1_gnn_all = _L1_gnn_setup()
    _L1_gnn_in = {k: v for k, v in _L1_gnn_all.items() if k in ('W', 'b', 'deg_coeff', 'coeff_param', 'scale_param')}
    del _L1_gnn_all
    return {'x': x, 'src': src, 'dst': dst, 'edge_attr_32': edge_attr_32, 'edge_weight': edge_weight, 'edge_weight_n2': edge_weight_n2, 'L0_gnn_Wf1': _L0_gnn_in['Wf1'], 'L0_gnn_bf1': _L0_gnn_in['bf1'], 'L0_gnn_Ws1': _L0_gnn_in['Ws1'], 'L0_gnn_bs1': _L0_gnn_in['bs1'], 'L0_gnn_gw1': _L0_gnn_in['gw1'], 'L0_gnn_gb1': _L0_gnn_in['gb1'], 'L0_gnn_gm1': _L0_gnn_in['gm1'], 'L0_gnn_Wf2': _L0_gnn_in['Wf2'], 'L0_gnn_bf2': _L0_gnn_in['bf2'], 'L0_gnn_Ws2': _L0_gnn_in['Ws2'], 'L0_gnn_bs2': _L0_gnn_in['bs2'], 'L0_gnn_gw2': _L0_gnn_in['gw2'], 'L0_gnn_gb2': _L0_gnn_in['gb2'], 'L0_gnn_gm2': _L0_gnn_in['gm2'], 'L1_gnn_W': _L1_gnn_in['W'], 'L1_gnn_b': _L1_gnn_in['b'], 'L1_gnn_deg_coeff': _L1_gnn_in['deg_coeff'], 'L1_gnn_coeff_param': _L1_gnn_in['coeff_param'], 'L1_gnn_scale_param': _L1_gnn_in['scale_param']}

def reference(x, src, dst, edge_attr_32, edge_weight, edge_weight_n2, L0_gnn_Wf1, L0_gnn_bf1, L0_gnn_Ws1, L0_gnn_bs1, L0_gnn_gw1, L0_gnn_gb1, L0_gnn_gm1, L0_gnn_Wf2, L0_gnn_bf2, L0_gnn_Ws2, L0_gnn_bs2, L0_gnn_gw2, L0_gnn_gb2, L0_gnn_gm2, L1_gnn_W, L1_gnn_b, L1_gnn_deg_coeff, L1_gnn_coeff_param, L1_gnn_scale_param):
    import jax
    import jax.numpy as jnp

    def _L0_gnn_ref(x, index, attr, batch, Wf1, bf1, Ws1, bs1, gw1, gb1, gm1, Wf2, bf2, Ws2, bs2, gw2, gb2, gm2):
        import jax, jax.numpy as jnp
        import numpy as np
        N = 12500
        E = 150000
        F = 64
        D = 32
        G = 64
        EPS = 1e-05
        NEG_SLOPE = 0.01

        def _cgconv(x, src, dst, attr, Wf, bf, Ws, bs):
            z = jnp.concatenate([x[dst], x[src], attr], axis=-1)
            m = jax.nn.sigmoid(z @ Wf + bf) * jax.nn.softplus(z @ Ws + bs)
            agg = jax.ops.segment_sum(m, dst, num_segments=N)
            return agg + x

        def _graph_norm(x, batch, w, b, ms):
            cnt = jax.ops.segment_sum(jnp.ones((N,), x.dtype), batch, num_segments=G)
            cnt = jnp.maximum(cnt, 1.0)[:, None]
            mean = jax.ops.segment_sum(x, batch, num_segments=G) / cnt
            out = x - mean[batch] * ms
            var = jax.ops.segment_sum(out * out, batch, num_segments=G) / cnt
            std = jnp.sqrt(var + EPS)
            return w * out / std[batch] + b

        def _leaky_relu(x):
            return jnp.where(x >= 0, x, NEG_SLOPE * x)
        src, dst = (index[0], index[1])
        h = _leaky_relu(_graph_norm(_cgconv(x, src, dst, attr, Wf1, bf1, Ws1, bs1), batch, gw1, gb1, gm1))
        h = _leaky_relu(_graph_norm(_cgconv(h, src, dst, attr, Wf2, bf2, Ws2, bs2), batch, gw2, gb2, gm2))
        return h

    def _L1_gnn_ref(h, edge_index, adj_v, deg_v, W, b, deg_coeff, coeff_param, scale_param):
        import jax, jax.numpy as jnp
        import numpy as np
        N, E, D_IN, D_OUT = (8192, 131072, 64, 64)
        EPS = 1e-08
        n_nodes = h.shape[0]
        Wh = h @ W + b
        row, col = (edge_index[0], edge_index[1])
        sc = jax.nn.softplus(deg_coeff[0] * deg_v + deg_coeff[1])
        Wr = Wh[row]
        Wc = Wh[col]
        dot = jnp.sum(Wr * Wc, axis=-1)
        nr = jnp.sqrt(jnp.sum(Wr * Wr, axis=-1))
        nc = jnp.sqrt(jnp.sum(Wc * Wc, axis=-1))
        sim = dot / jnp.maximum(nr * nc, EPS)
        sim_pos = jax.nn.relu(sim)
        sim_neg = -jax.nn.relu(-sim)
        no_diag = (row != col).astype(Wh.dtype)
        base = adj_v * sc * no_diag
        prop_pos = jax.ops.segment_sum((base * sim_pos)[:, None] * Wc, row, num_segments=n_nodes)
        prop_neg = jax.ops.segment_sum((base * sim_neg)[:, None] * Wc, row, num_segments=n_nodes)
        coeff = jax.nn.softmax(coeff_param)
        scale = jax.nn.softplus(scale_param)
        return scale * (coeff[0] * prop_pos + coeff[1] * prop_neg + coeff[2] * Wh)
    edge_index = jnp.stack([src, dst])
    batch0 = jnp.zeros((12500,), jnp.int32)
    x = _layernorm(x + _L0_gnn_ref(x, edge_index, edge_attr_32, batch0, L0_gnn_Wf1, L0_gnn_bf1, L0_gnn_Ws1, L0_gnn_bs1, L0_gnn_gw1, L0_gnn_gb1, L0_gnn_gm1, L0_gnn_Wf2, L0_gnn_bf2, L0_gnn_Ws2, L0_gnn_bs2, L0_gnn_gw2, L0_gnn_gb2, L0_gnn_gm2), axis=-1)
    x = _layernorm(x + _L1_gnn_ref(x, edge_index, edge_weight, edge_weight_n2, L1_gnn_W, L1_gnn_b, L1_gnn_deg_coeff, L1_gnn_coeff_param, L1_gnn_scale_param), axis=-1)
    return x

_drawn_inputs = setup_inputs


def setup_inputs(seed=0):
    import zlib

    import numpy as np

    out = dict(_drawn_inputs(seed))
    spreads = {'L0_gnn_gw1': (1.0, 0.2),
     'L0_gnn_gb1': (0.0, 0.337),
     'L0_gnn_gm1': (1.0, 0.2),
     'L0_gnn_gw2': (1.0, 0.2),
     'L0_gnn_gb2': (0.0, 0.1),
     'L0_gnn_gm2': (1.0, 0.2),
     'L1_gnn_coeff_param': (0.0, 0.279)}
    factors = {'edge_weight_n2': 3.626,
     'L0_gnn_bf1': 8.0,
     'L0_gnn_bs1': 8.0,
     'L0_gnn_bf2': 8.0,
     'L0_gnn_bs2': 8.0,
     'L1_gnn_b': 6.838}
    for name, (base, spread) in spreads.items():
        noise = np.random.default_rng([zlib.crc32(name.encode()), seed]).standard_normal(out[name].shape)
        drawn = base * np.exp(spread * noise) if base else spread * noise
        out[name] = jnp.asarray(drawn.astype(out[name].dtype))
    for name, factor in factors.items():
        out[name] = (out[name] * factor).astype(out[name].dtype)
    return out
```

```python
from contextlib import ExitStack

import numpy as np

import concourse.bass as bass
from concourse import mybir

P = 128
N, E, D, DA = 12500, 200000, 64, 32
TILES = 4
COLS = TILES * P
NT = -(-N // P)
NP = NT * P
GROUPS = 2 * (-(-E // (4 * COLS)))
PAIRS = GROUPS // 2
HALF = GROUPS * COLS
EP = 2 * HALF
SLOTS = 2 * TILES
CH = 7
CHUNKS = NT // CH
CP = CHUNKS // 2
CW = CH * D
SEARCH = 448
SC_COLS = 5
S_COLS = 100
SEARCHES = S_COLS // (2 * SC_COLS)
ACCS = 4
RUNS = SLOTS // ACCS
AROWS = NP + P
PADS_FROM = (N - (P - 1) * NT) * D
ZW = AROWS // P * D // 2
ZI = 49 * D
CLEARS = 2 * ACCS + 1 + EP // P * D // ZI
GATE_MIN = -44.0
EPS = 1e-5
SIM_EPS = 1e-8
SLOPE = 0.01

assert NT % (2 * CH) == 0 and SEARCH * SEARCH == EP and NT + 1 <= S_COLS and N > (P - 1) * NT

ALU = mybir.AluOpType
ACT = mybir.ActivationFunctionType
AX = mybir.AxisListType
F32 = mybir.dt.float32
I32 = mybir.dt.int32
BF16 = mybir.dt.bfloat16
ds = bass.ds


class Steps:

    def __init__(self, engine, sem):
        self.engine, self.sem, self.total, self.k, self.at = engine, sem, 0, 0, 0

    def begin(self, trip=0, per=0):
        self.at, self.k = self.total + trip * per, 0

    def end(self, trips=1, per=None):
        assert per is None or per == self.k, (per, self.k)
        self.total += trips * self.k
        self.at, self.k = self.total, 0

    def then(self, instruction):
        self.k += 1
        instruction.then_inc(self.sem, 1)
        self.engine.wait_ge(self.sem, self.at + self.k)


def gnn(nc, x, dst_rows, dst_blocks, dst_prev, block_last, seam_dst, src_g, src_e, dst_e, adj_e, deg_e,
        attr_t, conv, W, b, deg_coeff, coeff_param, scale_param, out):
    with ExitStack() as ctx:
        def sb(name, shape, dt=F32):
            return ctx.enter_context(nc.sbuf_tensor(name, shape, dt))

        def psum(name, shape):
            return ctx.enter_context(nc.psum_tensor(name, shape, F32))

        def sem(name):
            return ctx.enter_context(nc.semaphore(name))

        def two(name):
            return [sem(f"{name}_{i}") for i in range(2)]

        def dram(name, shape, dt=F32):
            return nc.dram_tensor(name, shape, dt).ap()

        inj_d = dram("first_edge_rows", [EP + P, D])
        sums_d = dram("running_sums", [EP + 1, D])
        same_d = dram("same_dst", [EP], BF16)
        h_d = dram("h_rows", [NP, D])
        wh_d = dram("wh_rows", [NP, D])
        acc_d = [dram(f"by_src_{a}", [AROWS, D]) for a in range(ACCS)]
        inj_groups = inj_d[0:EP].rearrange("(g p r) f -> g p (r f)", p=P, r=SLOTS)
        sums_groups = sums_d[0:EP].rearrange("(g p r) f -> g p (r f)", p=P, r=SLOTS)
        same_groups = same_d.rearrange("(g c) -> g c", c=COLS)

        ident = sb("ident", [P, P])
        ones = sb("ones", [P, P])
        before = sb("before", [P, P])
        zeros = sb("zeros", [P, ZW])
        node_id_i = sb("node_id_i", [P, S_COLS], I32)
        node_id = sb("node_id", [P, S_COLS])
        drop_i = sb("drop_i", [P, 2], I32)
        drop = sb("drop", [P, 2])
        w_dst = sb("w_dst", [P, 2, 2, P])
        w_src = sb("w_src", [P, 2, 2, P])
        w_attr = sb("w_attr", [2 * DA + 1, 2, 2, P])
        norm_w = sb("norm_w", [P, 2, 3, D])
        w_lin = sb("w_lin", [D + 1, D])
        coef_in = sb("coef_in", [P, 6])
        coef = sb("coef", [P, 16])
        last_idx = sb("last_idx", [P, NT])
        first_idx = sb("first_idx", [P, NT])
        seam = sb("seam", [P, NT])
        seam_idx = sb("seam_idx", [P, 1], I32)
        weight = sb("weight", [P, GROUPS * SLOTS])
        H = sb("H", [P, NT * D])
        X = sb("X", [P, NT * D])
        put_nodes = sb("put_nodes", [P, 2, CH], I32)
        get_nodes = sb("get_nodes", [P, 2, CH], I32)
        stage = sb("stage", [P, 2, CW])
        agg = sb("agg", [P, 2, CW])
        z = sb("z", [P, 2, CW])
        tmp = sb("tmp", [P, CW])
        total = sb("total", [P, CW])
        stat = sb("stat", [P, 8, D])
        small = sb("small", [P, 2, 5, CH])
        x2_t = sb("x2_t", [D + 1, 2, CH * P])
        seam_get = sb("seam_get", [P, D])
        seam_row = sb("seam_row", [P, D])
        idx = sb("idx", [P, 2, SLOTS], I32)
        inj = sb("inj", [P, 2, SLOTS * D])
        same = sb("same", [P, 2, COLS], BF16)
        attr = sb("attr", [2 * DA + 1, 2, COLS])
        G = sb("G", [P, 2, SLOTS * D])
        xd_t = sb("xd_t", [P, 2, COLS])

        arena = sb("arena", [P, 17600])

        def carve():
            at = [0]

            def tile(*shape, dt=F32):
                n = int(np.prod(shape))
                view = arena[:, at[0]:at[0] + n]
                at[0] += n
                if dt != F32:
                    view = view.bitcast(dt)
                names = "abc"[:len(shape)]
                sizes = dict(zip(names[1:], shape[1:]))
                return view.rearrange(f"p ({' '.join(names)}) -> p {' '.join(names)}", **sizes) if len(shape) > 1 else view
            return tile

        tile = carve()
        dst_now, dst_was, src_i, dst_i = (tile(GROUPS * SLOTS, dt=I32) for _ in range(4))
        deg, deg_tmp = tile(GROUPS * SLOTS), tile(GROUPS * SLOTS)
        last_i, last_f, junk = tile(SEARCH, dt=I32), tile(SEARCH), tile(SEARCH)
        block_rows = tile(2, SC_COLS, SEARCH, dt=I32)
        search = tile(2, 3, SC_COLS)
        block_of, first, valid = tile(S_COLS), tile(S_COLS), tile(NT)
        same_all = sb("same_all", [P, EP // P], BF16)
        block_idx = sb("block_idx", [P, 2, SC_COLS], I32)

        tile = carve()
        squares = tile(NT * D)
        xs_t = tile(2, COLS)
        gv = tile(2, 2, COLS)
        soft, msg = tile(COLS), tile(COLS)
        sum_t = tile(2, COLS)
        sums = tile(2, SLOTS * D)

        tile = carve()
        wc = tile(2, SLOTS * D)
        prod = tile(SLOTS * D)
        sq = tile(2 * SLOTS * D)
        dots = tile(12, SLOTS)
        src_f = tile(2, SLOTS)
        equal = tile(SLOTS, P)
        earlier = tile(SLOTS, P)
        w_msg = tile(SLOTS, D)
        put = tile(2, SLOTS * D)
        fin = tile(2, ACCS, CW)
        put_idx = sb("put_idx", [P, 2, SLOTS], I32)

        ps_inj = psum("ps_inj", [P, COLS])
        ps_g = psum("ps_g", [P, COLS])
        ps_gv = psum("ps_gv", [P, 2, 2, COLS])
        ps_out = psum("ps_out", [P, COLS])

        s_nodes = sem("x_loaded")
        s_search = sem("search_inputs_loaded")
        s_edges = sem("edge_scalars_loaded")
        s_weights = sem("weights_loaded")
        s_zeros = sem("zeros_set")
        s_tiles = sem("weight_tiles_zeroed")
        s_pool = sem("pool_constants")
        s_cleared = sem("tables_cleared")
        s_same_set = sem("same_set")
        s_same = sem("same_stored")
        s_dve = sem("dve_steps")
        s_act = sem("act_steps")
        s_ptick = sem("pool_waited")
        s_atick = sem("act_waited")
        s_petick = sem("pe_waited")
        s_bidx = sem("block_idx_ready")
        s_rows = two("block_rows_gathered")
        s_deg = sem("deg_ready")
        s_dega = sem("deg_activated")
        s_setup = sem("setup_done")
        s_pnodes = sem("put_nodes_ready")
        s_stage = sem("stage_ready")
        s_scat = sem("node_columns_scattered")
        s_table = two("chunk_stored")
        s_gnodes = sem("get_nodes_ready")
        s_agg = two("agg_gathered")
        s_part = sem("partition_sums")
        s_tot = sem("node_sums")
        s_var = sem("variance_ready")
        s_std = sem("std_ready")
        s_hcopy = sem("h_copied")
        s_seam = sem("seam_sums_loaded")
        s_sget = sem("seam_row_gathered")
        s_sput = sem("seam_row_put")
        s_pads = sem("padded_nodes_zeroed")
        s_lnv = sem("ln_variance_ready")
        s_lnr = sem("ln_root_ready")
        s_z = sem("x2_ready")
        s_zt = sem("x2_turned")
        s_ztc = sem("x2_turned_copied")
        s_wh = sem("wh_ready")
        s_whc = sem("wh_copied")
        s_fin = two("by_src_loaded")
        s_fused = sem("by_src_used")
        s_result = sem("result_ready")
        s_out_st = two("result_stored")
        s_idx = two("idx_loaded")
        s_load = two("group_loaded")
        s_gath = two("src_rows_gathered")
        s_injt = sem("inj_turned")
        s_scan = sem("dst_rows_carried")
        s_gt = sem("src_rows_turned")
        s_xs = sem("src_rows_copied")
        s_gates = sem("gates_ready")
        s_fold = sem("gates_clamped")
        s_soft = sem("softplus_ready")
        s_lns = sem("gates_activated")
        s_msg = sem("messages_ready")
        s_sumt = sem("messages_summed")
        s_turned = sem("sums_turned")
        s_sums = sem("sums_copied")
        s_stored = two("sums_stored")
        s_wt = sem("wc_turned")
        s_wc = sem("wc_copied")
        s_sq = sem("squares_ready")
        s_n2 = sem("norm_products_ready")
        s_nn = sem("norm_product_roots")
        s_used = sem("src_rows_used")
        s_srcf = sem("src_float")
        s_srcb = sem("src_spread")
        s_equal = sem("equal_ready")
        s_pidx = sem("put_idx_ready")
        s_wm = sem("weighted_ready")
        s_comb = sem("combined")
        s_put = sem("put_ready")
        s_added = [sem(f"added_{a}") for a in range(ACCS)]

        by_two = [s_bidx, s_pnodes, s_stage, s_gnodes, s_hcopy, s_lnv, s_lnr, s_z, s_zt, s_ztc, s_wh, s_whc,
                  s_fused, s_result, s_injt, s_scan, s_gt, s_xs, s_gates, s_fold, s_soft, s_lns, s_msg,
                  s_sumt, s_turned, s_sums, s_wt, s_wc, s_sq, s_n2, s_nn, s_used, s_srcf, s_srcb,
                  s_equal, s_pidx, s_wm, s_comb, s_put]
        by_sp = [s_table, s_out_st, s_stored]

        def done(rnd, h, buf, back=0):
            return h * 2 + (rnd * GROUPS + buf + 3 - back)

        def cdone(rnd, h, buf, back=0):
            return h * 2 + (rnd * CHUNKS + buf + 3 - back)

        def scattered(rnd, h, buf, column=CH):
            return h * (32 * CH) + 16 * (rnd * NT + buf * CH + column)

        def tabled(rnd, h, back=0):
            return h * 16 + 16 * (rnd * CP + 2 - back)

        def stored(rnd, h, back=0):
            return h * 16 + 16 * (rnd * PAIRS + 2 - back)

        def loaded(layer, h):
            return h * (64 if layer < 2 else 48) + (64 * layer * PAIRS + (64 if layer < 2 else 48))

        def gathered(layer, h):
            return h * (16 * SLOTS) + 16 * SLOTS * (layer * PAIRS + 1)

        def added(h, buf, run):
            return h * (32 * RUNS) + 16 * (buf * RUNS + run)

        def put_before(engine, h, buf):
            for a in range(ACCS):
                if not at_start(h):
                    engine.wait_ge(s_added[a], added(h, buf, 0) - 16 * RUNS)

        def at_start(h):
            return isinstance(h, int) and h == 0

        def all_trips(engine, body, trips):
            body(0)
            with engine.Fori(1, trips) as i:
                body(i)

        def chunk(h, buf):
            return ds(h * (2 * CW) + buf * CW, CW)

        def ccols(h, buf):
            return ds(h * (2 * CH) + buf * CH, CH)

        def nodes(ap):
            return ap.rearrange("(p t) f -> p (t f)", p=P)

        def by_node(ap):
            return ap.rearrange("p (c f) -> p c f", f=D)

        def across(ap, n):
            return ap.unsqueeze(1).to_broadcast([P, n, ap.shape[1]])

        def along(ap, n):
            return ap.unsqueeze(2).to_broadcast([P, ap.shape[1], n])

        def turned(ap, j):
            return ap.rearrange("p (q j) -> p q j", j=TILES)[:, :, j]

        def with_lag(engine, now, later, peeled=0):
            now(0, 0)
            for i in range(peeled):
                now(i, 1)
                later(i, 0)
                now(i + 1, 0)
                later(i, 1)
            with engine.Fori(peeled, PAIRS - 1) as i:
                now(i, 1)
                later(i, 0)
                now(i + 1, 0)
                later(i, 1)
            now(PAIRS - 1, 1)
            later(PAIRS - 1, 0)
            later(PAIRS - 1, 1)

        block = ctx.enter_context(nc.Block())

        @block.sync
        def _(sp):
            def load(out_, in_, s):
                sp.dma_start(out_, in_).then_inc(s, 16)

            load(last_i, block_last.to_broadcast([P, SEARCH]), s_search)
            load(dst_now, dst_rows, s_search)
            load(dst_was, dst_prev, s_search)
            load(X[:], nodes(x), s_nodes)
            load(H[:], nodes(x), s_nodes)
            load(dst_i, dst_e, s_edges)
            load(src_i, src_e, s_edges)
            load(weight[:], adj_e, s_edges)
            load(deg, deg_e, s_edges)
            load(seam_idx[:], seam_dst.to_broadcast([P, 1]), s_edges)
            load(coef_in[:, 0:2], deg_coeff.to_broadcast([P, 2]), s_edges)
            load(coef_in[:, 2:5], coeff_param.to_broadcast([P, 3]), s_edges)
            load(coef_in[:, 5:6], scale_param.to_broadcast([P, 1]), s_edges)
            sp.wait_ge(s_same_set, 1)
            load(same_d.rearrange("(p c) -> p c", p=P), same_all[:], s_same)
            sp.wait_ge(s_tiles, 1)
            for layer, (Wf, bf, Ws, bs, gw, gb, gm) in enumerate(conv):
                for k, (w, bias) in enumerate(((Wf, bf), (Ws, bs))):
                    for s in range(2):
                        o = slice(s * D, (s + 1) * D)
                        load(w_dst[o, layer, k, o], w[0:D, :], s_weights)
                        load(w_src[o, layer, k, o], w[D:2 * D, :], s_weights)
                        load(w_attr[s * DA:(s + 1) * DA, layer, k, o], w[2 * D:, :], s_weights)
                        load(w_attr[2 * DA:2 * DA + 1, layer, k, o], bias, s_weights)
                for k, v in enumerate((gw, gb, gm)):
                    load(norm_w[:, layer, k, :], v.to_broadcast([P, D]), s_weights)
            load(w_lin[0:D, :], W, s_weights)
            load(w_lin[D:D + 1, :], b, s_weights)
            sp.wait_ge(s_same, 16)

            for layer in range(3):
                sp.wait_ge(s_scat, 16 * NT * (layer + 1))
                sp.wait_ge(s_sget, 16 * (layer + 1))
                load(inj_d[1:2, :], seam_get[0:1, :], s_sput)
                sp.wait_ge(s_sput, 16 * (layer + 1))

                def load_group(h, buf):
                    g = h * 2 + buf
                    if layer < 2:
                        sp.wait_ge(s_gt, done(layer, h, buf, 2))
                    else:
                        sp.wait_ge(s_used, done(0, h, buf, 2))
                    load(idx[:, buf], src_g[:, ds(g * SLOTS, SLOTS)], s_idx[buf])
                    sp.wait_ge(s_scan, done(layer, h, buf, 2))
                    load(inj[:, buf], inj_groups[ds(g, 1)].rearrange("a p c -> p (a c)"), s_load[buf])
                    if layer < 2:
                        sp.wait_ge(s_sumt, done(layer, h, buf, 2))
                    for s in range(2):
                        load(same[s * D:(s + 1) * D, buf],
                             same_groups[ds(g + s * GROUPS, 1), :].to_broadcast([D, COLS]), s_load[buf])
                    if layer < 2:
                        sp.wait_ge(s_gates, done(layer, h, buf, 2))
                        load(attr[0:2 * DA, buf], attr_t[ds(g, 1)].rearrange("a k c -> k (a c)"), s_load[buf])

                def store_sums(h, buf):
                    g = h * 2 + buf
                    sp.wait_ge(s_sums, done(layer, h, buf))
                    load(sums_groups[ds(g, 1)].rearrange("a p c -> p (a c)"), sums[:, buf], s_stored[buf])

                load_group(0, 0)
                load_group(0, 1)
                with sp.Fori(1, PAIRS) as i:
                    for buf in range(2):
                        load_group(i, buf)
                        if layer < 2:
                            store_sums(i - 1, buf)
                if layer == 2:
                    break
                for buf in range(2):
                    store_sums(PAIRS - 1, buf)
                for buf in range(2):
                    sp.wait_ge(s_stored[buf], stored(layer, PAIRS - 1))
                load(seam_row[:], sums_d[EP - 2:EP - 1, :].to_broadcast([P, D]), s_seam)
                table_out = nodes((h_d, wh_d)[layer])
                with sp.Fori(0, CP) as i:
                    for buf in range(2):
                        sp.wait_ge(s_stage, cdone(layer + 1, i, buf))
                        load(table_out[:, chunk(i, buf)], stage[:, buf], s_table[buf])
                if layer == 0:
                    sp.wait_ge(s_hcopy, cdone(0, CP - 1, 1))
                    load(H[P - 1:P, PADS_FROM:NT * D], zeros[0:1, 0:NT * D - PADS_FROM], s_pads)

            for a in range(ACCS):
                sp.wait_ge(s_added[a], 16 * GROUPS * RUNS)
            with sp.Fori(0, CP) as i:
                for buf in range(2):
                    sp.wait_ge(s_fused, cdone(0, i, buf, 2))
                    for a in range(ACCS):
                        load(fin[:, buf, a], nodes(acc_d[a][0:NP])[:, chunk(i, buf)], s_fin[buf])
                for buf in range(2):
                    sp.wait_ge(s_result, cdone(0, i, buf))
                    load(nodes(out)[:, chunk(i, buf)], z[:, buf], s_out_st[buf])
            for buf in range(2):
                sp.wait_ge(s_out_st[buf], 16 * (CP + 1))

        @block.gpsimd
        def _(pool):
            pool.memset(ident[:], 0.0).then_inc(s_pool, 1)
            pool.memset(before[:], 1.0).then_inc(s_pool, 1)
            pool.wait_ge(s_pool, 2)
            pool.affine_select(out=ident[:], in_=ident[:], compare_op=ALU.not_equal, fill=1.0, base=0,
                               pattern=[[-1, P]], channel_multiplier=1).then_inc(s_pool, 1)
            pool.affine_select(out=before[:], in_=before[:], compare_op=ALU.is_gt, fill=0.0, base=0,
                               pattern=[[-1, P]], channel_multiplier=1).then_inc(s_pool, 1)
            pool.iota(node_id_i[:], pattern=[[1, S_COLS]], base=0, channel_multiplier=NT).then_inc(s_pool, 1)
            pool.iota(drop_i[:, 0:1], pattern=[[1, 1]], base=EP, channel_multiplier=1).then_inc(s_pool, 1)
            pool.iota(drop_i[:, 1:2], pattern=[[1, 1]], base=NP, channel_multiplier=1).then_inc(s_pool, 1)

            def wait(s, value):
                pool.wait_ge(s, value)
                pool.sem_inc(s_ptick, 1)

            def gather(out_, table_in, index, s):
                pool.indirect_dma_start(out_, None, table_in, bass.IndirectOffsetOnAxis(ap=index, axis=0)).then_inc(s, 16)

            with pool.Fori(0, SEARCHES) as i:
                for buf in range(2):
                    wait(s_bidx, cdone(0, i, buf))
                    for c in range(SC_COLS):
                        gather(block_rows[:, buf, c], dst_blocks, block_idx[:, buf, c:c + 1], s_rows[buf])

            for layer in range(3):
                if layer == 0:
                    pool.wait_ge(s_cleared, 16 * CLEARS)
                def put_rows(h):
                    for buf in range(2):
                        wait(s_pnodes, cdone(layer, h, buf))
                        wait(s_stage, cdone(layer, h, buf))
                        for c in range(CH):
                            if layer or buf or c or not at_start(h):
                                wait(s_scat, scattered(layer, h, buf, c))
                            pool.indirect_dma_start(
                                inj_d, bass.IndirectOffsetOnAxis(ap=put_nodes[:, buf, c:c + 1], axis=0),
                                stage[:, buf, c * D:(c + 1) * D], None).then_inc(s_scat, 16)

                all_trips(pool, put_rows, CP)
                table_in = (x, h_d, wh_d)[layer]
                if layer:
                    for buf in range(2):
                        pool.wait_ge(s_table[buf], tabled(layer - 1, CP - 1))
                else:
                    pool.wait_ge(s_edges, 16 * 8)
                if layer:
                    pool.wait_ge(s_sput, 16 * layer)
                gather(seam_get[:], table_in, seam_idx[:], s_sget)

                def gather_group(h, buf):
                    wait(s_idx[buf], h * 16 + 16 * (layer * PAIRS + 1))
                    if layer < 2:
                        wait(s_gt, done(layer, h, buf, 2))
                    else:
                        wait(s_used, done(0, h, buf, 2))
                    for k in range(SLOTS):
                        gather(G[:, buf, k * D:(k + 1) * D], table_in, idx[:, buf, k:k + 1], s_gath[buf])

                def add_group(h, buf):
                    wait(s_pidx, done(0, h, buf))
                    wait(s_put, done(0, h, buf))
                    for k in range(SLOTS):
                        a = k % ACCS
                        if k >= ACCS or buf or not at_start(h):
                            wait(s_added[a], added(h, buf, k // ACCS))
                        pool.indirect_dma_start(
                            acc_d[a], bass.IndirectOffsetOnAxis(ap=put_idx[:, buf, k:k + 1], axis=0),
                            put[:, buf, k * D:(k + 1) * D], None, compute_op=ALU.add).then_inc(s_added[a], 16)

                if layer == 2:
                    with_lag(pool, gather_group, add_group, peeled=1)
                    break
                with pool.Fori(0, PAIRS) as i:
                    for buf in range(2):
                        gather_group(i, buf)
                for buf in range(2):
                    pool.wait_ge(s_stored[buf], stored(layer, PAIRS - 1))
                with pool.Fori(0, CP) as i:
                    for buf in range(2):
                        wait(s_gnodes, cdone(layer, i, buf))
                        for c in range(CH):
                            gather(agg[:, buf, c * D:(c + 1) * D], sums_d, get_nodes[:, buf, c:c + 1], s_agg[buf])

        @block.tensor
        def _(pe):
            pe.wait_ge(s_pool, 7)
            pe.wait_ge(s_weights, 16 * (2 * 19 + 2))

            def turn_inj(layer, h, buf):
                pe.wait_ge(s_load[buf], loaded(layer, h))
                pe.wait_ge(s_scan, done(layer, h, buf, 1))
                for j in range(TILES):
                    mm = pe.transpose(turned(ps_inj, j), inj[:, buf, j * P:(j + 1) * P], ident[:])
                mm.then_inc(s_injt, 1)

            for layer in range(2):
                def now(h, buf):
                    turn_inj(layer, h, buf)
                    pe.wait_ge(s_gath[buf], gathered(layer, h))
                    pe.wait_ge(s_xs, done(layer, h, buf, 1))
                    for j in range(TILES):
                        mm = pe.transpose(turned(ps_g, j), G[:, buf, j * P:(j + 1) * P], ident[:])
                    mm.then_inc(s_gt, 1)
                    pe.wait_ge(s_soft, done(layer, h, buf, 2))
                    for k in range(2):
                        pe.matmul(ps_gv[:, buf, k], w_attr[:, layer, k], attr[:, buf], start=True, stop=False)
                    pe.wait_ge(s_xs, done(layer, h, buf))
                    for k in range(2):
                        pe.matmul(ps_gv[:, buf, k], w_src[:, layer, k], xs_t[:, buf], start=False, stop=False)
                    pe.wait_ge(s_scan, done(layer, h, buf))
                    for k in range(2):
                        mm = pe.matmul(ps_gv[:, buf, k], w_dst[:, layer, k], xd_t[:, buf], start=False, stop=True)
                    mm.then_inc(s_gates, 1)

                def later(h, buf):
                    pe.wait_ge(s_sumt, done(layer, h, buf))
                    pe.wait_ge(s_sums, done(layer, h, buf, 1))
                    for j in range(TILES):
                        mm = pe.transpose(ps_out[:, j * P:(j + 1) * P], turned(sum_t[:, buf], j), ident[:])
                    mm.then_inc(s_turned, 1)

                with_lag(pe, now, later)
                pe.wait_ge(s_part, 2 * layer + 1)
                pe.matmul(ps_out[:, 0:CW], ones[:], total[:], start=True, stop=True).then_inc(s_tot, 1)
                pe.wait_ge(s_part, 2 * layer + 2)
                pe.matmul(ps_out[:, 0:D], ones[:], stat[:, 2], start=True, stop=True).then_inc(s_tot, 1)

            with pe.Fori(0, CP) as i:
                for buf in range(2):
                    pe.wait_ge(s_z, cdone(0, i, buf))
                    pe.wait_ge(s_ztc, cdone(0, i, buf, 1))
                    pe.sem_inc(s_petick, 1)
                    for c in range(CH):
                        mm = pe.transpose(ps_gv[0:D, 0, c // TILES, c % TILES * P:(c % TILES + 1) * P],
                                          z[:, buf, c * D:(c + 1) * D], ident[:])
                    mm.then_inc(s_zt, 1)
                    pe.wait_ge(s_ztc, cdone(0, i, buf))
                    pe.wait_ge(s_whc, cdone(0, i, buf, 1))
                    for c in range(CH):
                        mm = pe.matmul(ps_out[:, c * D:(c + 1) * D], x2_t[:, buf, c * P:(c + 1) * P], w_lin[:],
                                       start=True, stop=True)
                    mm.then_inc(s_wh, 1)

            spread = ps_gv.rearrange("p b k (t e) -> p b (k t) e", e=P)
            with pe.Fori(0, PAIRS) as i:
                for buf in range(2):
                    turn_inj(2, i, buf)
                    pe.wait_ge(s_srcf, done(0, i, buf))
                    pe.wait_ge(s_equal, done(0, i, buf, 2))
                    for k in range(SLOTS):
                        mm = pe.transpose(spread[:, buf, k], src_f[:, buf, k:k + 1].to_broadcast([P, P]), ident[:])
                    mm.then_inc(s_srcb, 1)
                    pe.wait_ge(s_scan, done(2, i, buf))
                    pe.wait_ge(s_sq, done(0, i, buf, 1))
                    for j in range(TILES):
                        mm = pe.transpose(ps_g[:, j * P:(j + 1) * P], turned(xd_t[:, buf], j), ident[:])
                    mm.then_inc(s_wt, 1)
                    pe.wait_ge(s_equal, done(0, i, buf))
                    pe.wait_ge(s_wm, done(0, i, buf))
                    pe.wait_ge(s_put, done(0, i, buf, 1))
                    for k in range(SLOTS):
                        mm = pe.matmul(ps_out[:, k * D:(k + 1) * D], equal[:, k], w_msg[:, k], start=True, stop=True)
                    mm.then_inc(s_comb, 1)

        @block.scalar
        def _(act):
            steps = Steps(act, s_act)
            act.wait_ge(s_zeros, 1)
            for a in range(ACCS):
                rows_a = acc_d[a].rearrange("(p r) f -> p (r f)", p=P)
                for k in range(2):
                    act.dma_start(rows_a[:, k * ZW:(k + 1) * ZW], zeros[:]).then_inc(s_cleared, 16)
            act.dma_start(sums_d[EP:EP + 1, :], zeros[0:1, 0:D]).then_inc(s_cleared, 16)
            inj_rows = inj_d[0:EP].rearrange("(p r) f -> p (r f)", p=P)
            with act.Fori(0, EP // P * D // ZI) as i:
                act.dma_start(inj_rows[:, ds(i * ZI, ZI)], zeros[:, 0:ZI]).then_inc(s_cleared, 16)

            def wait(s, value):
                act.wait_ge(s, value)
                act.sem_inc(s_atick, 1)

            act.wait_ge(s_deg, 1)
            steps.begin()
            steps.then(nc.scalar.activation(deg_tmp, deg_tmp, ACT.Exp))
            steps.then(nc.scalar.activation(coef[:, 0:4], coef[:, 0:4], ACT.Exp))
            steps.then(nc.scalar.activation(coef[:, 3:4], coef[:, 3:4], ACT.Ln, bias=1.0))
            nc.scalar.activation(deg_tmp, deg_tmp, ACT.Ln, bias=1.0).then_inc(s_dega, 1)
            steps.end()

            act.wait_ge(s_setup, 1)
            for layer in range(2):
                def now(h, buf):
                    act.wait_ge(s_gt, done(layer, h, buf))
                    act.wait_ge(s_gates, done(layer, h, buf, 2))
                    nc.scalar.copy(xs_t[:, buf], ps_g[:]).then_inc(s_xs, 1)
                    act.wait_ge(s_gates, done(layer, h, buf))
                    act.wait_ge(s_msg, done(layer, h, buf, 2))
                    steps.then(nc.scalar.activation(gv[:, buf, 1], ps_gv[:, buf, 1], ACT.Abs))
                    act.wait_ge(s_fold, done(layer, h, buf))
                    both = gv[:, buf].rearrange("p k c -> p (k c)")
                    steps.then(nc.scalar.activation(both, both, ACT.Exp, scale=-1.0))
                    steps.then(nc.scalar.activation(both, both, ACT.Ln, bias=1.0))
                    nc.scalar.activation(both[:, 0:COLS], both[:, 0:COLS], ACT.Exp, scale=-1.0).then_inc(s_lns, 1)

                def later(h, buf):
                    act.wait_ge(s_turned, done(layer, h, buf))
                    act.wait_ge(s_stored[buf], stored(layer, h, 1))
                    nc.scalar.copy(sums[:, buf], ps_out[:]).then_inc(s_sums, 1)

                steps.begin()
                now(0, 0)
                steps.end()
                with act.Fori(0, PAIRS - 1) as i:
                    steps.begin(i, 6)
                    now(i, 1)
                    later(i, 0)
                    now(i + 1, 0)
                    later(i, 1)
                steps.end(PAIRS - 1, 6)
                steps.begin()
                now(PAIRS - 1, 1)
                later(PAIRS - 1, 0)
                later(PAIRS - 1, 1)
                steps.end()

                act.wait_ge(s_var, layer + 1)
                nc.scalar.activation(stat[:, 4], stat[:, 4], ACT.Sqrt).then_inc(s_std, 1)
                if layer == 0:
                    with act.Fori(0, CP) as i:
                        for buf in range(2):
                            wait(s_stage, cdone(1, i, buf))
                            nc.scalar.copy(H[:, chunk(i, buf)], stage[:, buf]).then_inc(s_hcopy, 1)
                    continue
                with act.Fori(0, CP) as i:
                    for buf in range(2):
                        act.wait_ge(s_lnv, cdone(0, i, buf))
                        nc.scalar.activation(small[:, buf, 2], small[:, buf, 2], ACT.Sqrt).then_inc(s_lnr, 1)
                        wait(s_z, cdone(0, i, buf))
                        nc.scalar.copy(H[:, chunk(i, buf)], z[:, buf]).then_inc(s_hcopy, 1)
                        act.wait_ge(s_zt, cdone(0, i, buf))
                        act.wait_ge(s_wh, cdone(0, i, buf, 2))
                        for k, n in ((0, TILES * P), (1, (CH - TILES) * P)):
                            c = nc.scalar.copy(x2_t[0:D, buf, k * COLS:k * COLS + n], ps_gv[0:D, 0, k, 0:n])
                        c.then_inc(s_ztc, 1)
                        act.wait_ge(s_wh, cdone(0, i, buf))
                        act.wait_ge(s_scat, scattered(2, i, buf - 1))
                        act.wait_ge(s_table[buf], tabled(1, i, 1))
                        nc.scalar.copy(stage[:, buf], ps_out[:, 0:CW]).then_inc(s_stage, 1)
                        nc.scalar.copy(X[:, chunk(i, buf)], ps_out[:, 0:CW]).then_inc(s_whc, 1)

            def last_layer(i):
                for buf in range(2):
                    act.wait_ge(s_wt, done(0, i, buf))
                    act.wait_ge(s_wm, done(0, i, buf, 2))
                    nc.scalar.copy(wc[:, buf], ps_g[:]).then_inc(s_wc, 1)
                    act.wait_ge(s_n2, done(0, i, buf, 1))
                    nc.scalar.activation(sq[:, 0:SLOTS * D], ps_g[:], ACT.Square)
                    act.wait_ge(s_gath[buf], gathered(2, i))
                    nc.scalar.activation(sq[:, SLOTS * D:], G[:, buf], ACT.Square).then_inc(s_sq, 1)
                    act.wait_ge(s_n2, done(0, i, buf))
                    nc.scalar.activation(dots[:, 3], dots[:, 3], ACT.Sqrt).then_inc(s_nn, 1)
                    act.wait_ge(s_comb, done(0, i, buf))
                    put_before(act, i, buf)
                    nc.scalar.copy(put[:, buf], ps_out[:]).then_inc(s_put, 1)

            all_trips(act, last_layer, PAIRS)

            with act.Fori(0, CP) as i:
                for buf in range(2):
                    act.wait_ge(s_lnv, cdone(1, i, buf))
                    nc.scalar.activation(small[:, buf, 2], small[:, buf, 2], ACT.Sqrt).then_inc(s_lnr, 1)

        @block.vector
        def _(dve):
            v = nc.vector
            steps = Steps(dve, s_dve)
            then = steps.then
            v.memset(zeros[:], 0.0).then_inc(s_zeros, 1)
            for s in by_two:
                dve.sem_inc(s, 2)
            for pair in by_sp:
                for s in pair:
                    dve.sem_inc(s, 16)
            for t in (w_dst, w_src):
                v.memset(t[:], 0.0)
            v.memset(w_attr[:], 0.0).then_inc(s_tiles, 1)
            v.memset(ones[:], 1.0)
            v.memset(attr[2 * DA:2 * DA + 1], 1.0)
            v.memset(x2_t[D:D + 1], 1.0)
            steps.begin()
            then(v.memset(xd_t[:, 1, COLS - 1:COLS], 0.0))
            dve.wait_ge(s_search, 48)
            v.tensor_tensor(same_all[:], dst_now, dst_was, ALU.is_equal).then_inc(s_same_set, 1)
            then(v.tensor_copy(last_f, last_i))
            dve.wait_ge(s_pool, 7)
            then(v.tensor_copy(node_id[:], node_id_i[:]))
            then(v.tensor_copy(drop[:], drop_i[:]))
            steps.end()


            def find_block(h, buf):
                at = ds(h * (2 * SC_COLS) + buf * SC_COLS, SC_COLS)
                then(v.tensor_scalar(search[:, buf, 0], node_id[:, at], 0.0, None, ALU.add))
                for c in range(SC_COLS):
                    then(v.tensor_scalar(junk, last_f, search[:, buf, 0, c:c + 1], 0.0, ALU.is_lt, ALU.add,
                                         accum_out=search[:, buf, 1, c:c + 1]))
                then(v.tensor_scalar(search[:, buf, 2], search[:, buf, 1], float(SEARCH - 1), None, ALU.min))
                v.tensor_scalar(block_idx[:, buf], search[:, buf, 2], 0.0, None, ALU.add).then_inc(s_bidx, 1)

            def find_edge(h, buf):
                dve.wait_ge(s_rows[buf], h * (16 * SC_COLS) + 16 * SC_COLS)
                for c in range(SC_COLS):
                    then(v.tensor_scalar(junk, block_rows[:, buf, c], search[:, buf, 0, c:c + 1], 0.0, ALU.is_lt,
                                         ALU.add, accum_out=search[:, buf, 1, c:c + 1]))
                then(v.scalar_tensor_tensor(first[:, ds(h * (2 * SC_COLS) + buf * SC_COLS, SC_COLS)], search[:, buf, 2],
                                            float(SEARCH), search[:, buf, 1], ALU.mult, ALU.add))

            def lagged(now, later, trips, per):
                steps.begin()
                now(0, 0)
                steps.end()
                with dve.Fori(0, trips - 1) as i:
                    steps.begin(i, per)
                    now(i, 1)
                    later(i, 0)
                    now(i + 1, 0)
                    later(i, 1)
                steps.end(trips - 1, per)
                steps.begin()
                now(trips - 1, 1)
                later(trips - 1, 0)
                later(trips - 1, 1)
                steps.end()

            lagged(find_block, find_edge, SEARCHES, 26)

            steps.begin()
            f, e = first[:, 0:NT], first[:, 1:NT + 1]
            then(v.tensor_tensor(valid, e, f, ALU.is_gt))
            then(v.scalar_tensor_tensor(valid, node_id[:, 0:NT], float(N), valid, ALU.is_lt, ALU.mult))
            row = squares[:, 0:NT]
            then(v.tensor_scalar(row, f, float(HALF), float(EP - 1), ALU.is_ge, ALU.mult))
            then(v.scalar_tensor_tensor(row, f, 2.0, row, ALU.mult, ALU.subtract))
            then(v.scalar_tensor_tensor(first_idx[:], row, drop[:, 0:1], valid, ALU.subtract, ALU.mult))
            then(v.tensor_scalar(first_idx[:], first_idx[:], drop[:, 0:1], None, ALU.add))
            then(v.tensor_scalar(row, e, float(HALF), float(EP - 1), ALU.is_gt, ALU.mult))
            then(v.scalar_tensor_tensor(row, e, 2.0, row, ALU.mult, ALU.subtract))
            then(v.scalar_tensor_tensor(last_idx[:], row, float(EP + 2), valid, ALU.subtract, ALU.mult))
            then(v.tensor_scalar(last_idx[:], last_idx[:], float(EP), None, ALU.add))
            then(v.tensor_scalar(seam[:], f, float(HALF), None, ALU.is_lt))
            then(v.scalar_tensor_tensor(seam[:], e, float(HALF), seam[:], ALU.is_gt, ALU.mult))

            dve.wait_ge(s_edges, 16 * 8)
            then(v.tensor_scalar(deg, deg, coef_in[:, 0:1], coef_in[:, 1:2], ALU.mult, ALU.add))
            then(v.scalar_tensor_tensor(deg_tmp, deg, -1.0, deg, ALU.mult, ALU.min))
            then(v.tensor_reduce(coef[:, 4:5], coef_in[:, 2:5], AX.X, ALU.max))
            then(v.tensor_scalar(coef[:, 0:3], coef_in[:, 2:5], coef[:, 4:5], None, ALU.subtract))
            v.scalar_tensor_tensor(coef[:, 3:4], coef_in[:, 5:6], -1.0, coef_in[:, 5:6], ALU.mult,
                                   ALU.min).then_inc(s_deg, 1)
            steps.end()

            dve.wait_ge(s_nodes, 32)

            def stage_idx(rnd, h, buf):
                if rnd or not at_start(h):
                    dve.wait_ge(s_scat, scattered(rnd, h, buf - 1))
                v.tensor_scalar(put_nodes[:, buf], first_idx[:, ccols(h, buf)], 0.0, None,
                                ALU.add).then_inc(s_pnodes, 1)

            def stage_x(h):
                for buf in range(2):
                    stage_idx(0, h, buf)
                    v.tensor_scalar(stage[:, buf], X[:, chunk(h, buf)], 1.0, None, ALU.mult).then_inc(s_stage, 1)

            all_trips(dve, stage_x, CP)

            steps.begin()
            dve.wait_ge(s_dega, 1)
            then(v.scalar_tensor_tensor(deg, deg, 0.0, deg_tmp, ALU.max, ALU.add))
            then(v.tensor_tensor(deg_tmp, src_i, dst_i, ALU.not_equal))
            then(v.tensor_tensor(weight[:], weight[:], deg, ALU.mult))
            then(v.tensor_tensor(weight[:], weight[:], deg_tmp, ALU.mult))
            then(v.scalar_tensor_tensor(coef[:, 5:6], coef_in[:, 5:6], 0.0, coef[:, 3:4], ALU.max, ALU.add))
            then(v.tensor_reduce(coef[:, 6:7], coef[:, 0:3], AX.X, ALU.add))
            then(v.reciprocal(coef[:, 7:8], coef[:, 6:7]))
            then(v.tensor_tensor(coef[:, 7:8], coef[:, 7:8], coef[:, 5:6], ALU.mult))
            then(v.tensor_scalar(coef[:, 8:11], coef[:, 0:3], coef[:, 7:8], None, ALU.mult))
            then(v.memset(sum_t[:, 1, COLS - 1:COLS], 0.0))
            dve.sem_inc(s_setup, 1)
            steps.end()

            def carry_dst(layer, h, buf):
                dve.wait_ge(s_injt, done(layer, h, buf))
                dve.wait_ge(s_load[buf], loaded(layer, h))
                if layer < 2:
                    dve.wait_ge(s_gates, done(layer, h, buf, 2))
                else:
                    dve.wait_ge(s_wt, done(0, h, buf, 2))
                dve.wait_ge(s_scan, done(layer, h, buf, 1))
                v.tensor_tensor_scan(xd_t[:, buf], same[:, buf], ps_inj[:], xd_t[:, 1 - buf, COLS - 1:COLS],
                                     ALU.mult, ALU.add).then_inc(s_scan, 1)

            def layer_norm(t, rnd, h, buf):
                m = small[:, buf]
                then(v.tensor_reduce(m[:, 0], by_node(t), AX.X, ALU.add))
                then(v.tensor_scalar(m[:, 1], m[:, 0], -1.0 / D, None, ALU.mult))
                then(v.tensor_tensor(t, by_node(t), along(m[:, 1], D), ALU.add))
                then(v.tensor_tensor(tmp[:], t, t, ALU.mult))
                then(v.tensor_reduce(m[:, 3], by_node(tmp[:]), AX.X, ALU.add))
                v.tensor_scalar(m[:, 2], m[:, 3], 1.0 / D, EPS, ALU.mult, ALU.add).then_inc(s_lnv, 1)
                dve.wait_ge(s_lnr, cdone(rnd, h, buf))
                then(v.reciprocal(m[:, 4], m[:, 2]))
                return v.tensor_tensor(t, by_node(t), along(m[:, 4], D), ALU.mult)

            for layer in range(2):
                def now(h, buf):
                    carry_dst(layer, h, buf)

                def fold(h, buf):
                    dve.wait_ge(s_gates, done(layer, h, buf))
                    v.tensor_scalar(gv[:, buf, 0], ps_gv[:, buf, 0], GATE_MIN, None, ALU.max).then_inc(s_fold, 1)

                def messages(h, buf):
                    dve.wait_ge(s_lns, done(layer, h, buf))
                    v.scalar_tensor_tensor(soft, ps_gv[:, buf, 1], 0.0, gv[:, buf, 1], ALU.max,
                                           ALU.add).then_inc(s_soft, 1)
                    dve.wait_ge(s_soft, done(layer, h, buf))
                    v.tensor_tensor(msg, gv[:, buf, 0], soft, ALU.mult).then_inc(s_msg, 1)
                    dve.wait_ge(s_msg, done(layer, h, buf))
                    dve.wait_ge(s_turned, done(layer, h, buf, 2))
                    dve.wait_ge(s_sumt, done(layer, h, buf, 1))
                    v.tensor_tensor_scan(sum_t[:, buf], same[:, buf], msg, sum_t[:, 1 - buf, COLS - 1:COLS],
                                         ALU.mult, ALU.add).then_inc(s_sumt, 1)

                now(0, 0)
                fold(0, 0)
                with dve.Fori(0, PAIRS - 1) as i:
                    now(i, 1)
                    messages(i, 0)
                    fold(i, 1)
                    now(i + 1, 0)
                    messages(i, 1)
                    fold(i + 1, 0)
                now(PAIRS - 1, 1)
                messages(PAIRS - 1, 0)
                fold(PAIRS - 1, 1)
                messages(PAIRS - 1, 1)

                def stage_get(h, buf):
                    v.tensor_scalar(get_nodes[:, buf], last_idx[:, ccols(h, buf)], 0.0, None,
                                    ALU.add).then_inc(s_gnodes, 1)

                def add_sums(h, buf):
                    hc = H[:, chunk(h, buf)]
                    then(v.tensor_tensor(by_node(tmp[:]), along(seam[:, ccols(h, buf)], D),
                                         across(seam_row[:], CH), ALU.mult))
                    dve.wait_ge(s_agg[buf], h * (16 * CH) + 16 * CH * (layer * CP + 1))
                    then(v.tensor_tensor(hc, hc, agg[:, buf], ALU.add))
                    then(v.tensor_tensor(hc, hc, tmp[:], ALU.add))
                    then(v.tensor_tensor(total[:], total[:], hc, ALU.add))

                dve.wait_ge(s_seam, 16 * (layer + 1))
                if layer:
                    dve.wait_ge(s_pads, 16)
                steps.begin()
                then(v.memset(total[:], 0.0))
                stage_get(0, 0)
                stage_get(0, 1)
                steps.end()
                with dve.Fori(0, CP - 1) as i:
                    steps.begin(i, 8)
                    for buf in range(2):
                        add_sums(i, buf)
                        stage_get(i + 1, buf)
                steps.end(CP - 1, 8)
                steps.begin()
                for buf in range(2):
                    add_sums(CP - 1, buf)
                dve.sem_inc(s_part, 1)
                dve.wait_ge(s_tot, 2 * layer + 1)
                then(v.tensor_reduce(stat[:, 0], ps_out[:, 0:CW].rearrange("p (c f) -> p f c", f=D), AX.X, ALU.add))
                then(v.scalar_tensor_tensor(stat[:, 1], stat[:, 0], -1.0 / N, norm_w[:, layer, 2], ALU.mult, ALU.mult))
                then(v.tensor_tensor(by_node(H[:]), by_node(H[:]), across(stat[:, 1], NT), ALU.add))
                then(v.tensor_tensor(squares, H[:], H[:], ALU.mult))
                v.tensor_reduce(stat[:, 2], squares.rearrange("p (t f) -> p f t", f=D), AX.X,
                                ALU.add).then_inc(s_part, 1)
                dve.wait_ge(s_tot, 2 * layer + 2)
                then(v.tensor_tensor(stat[:, 3], stat[:, 1], stat[:, 1], ALU.mult))
                then(v.scalar_tensor_tensor(stat[:, 3], stat[:, 3], float(N - NP), ps_out[:, 0:D], ALU.mult, ALU.add))
                v.tensor_scalar(stat[:, 4], stat[:, 3], 1.0 / N, EPS, ALU.mult, ALU.add).then_inc(s_var, 1)
                dve.wait_ge(s_std, layer + 1)
                then(v.reciprocal(stat[:, 5], stat[:, 4]))
                then(v.tensor_tensor(stat[:, 6], stat[:, 5], norm_w[:, layer, 0], ALU.mult))
                steps.end()

                with dve.Fori(0, CP) as i:
                    steps.begin(i, 4 if layer == 0 else 20)
                    for buf in range(2):
                        hc = H[:, chunk(i, buf)]
                        stage_idx(layer + 1, i, buf)
                        then(v.tensor_tensor(by_node(tmp[:]), by_node(hc), across(stat[:, 6], CH), ALU.mult))
                        then(v.tensor_tensor(by_node(tmp[:]), by_node(tmp[:]), across(norm_w[:, layer, 1], CH), ALU.add))
                        if layer == 0:
                            dve.wait_ge(s_table[buf], tabled(0, i, 1))
                            dve.wait_ge(s_hcopy, cdone(0, i, buf, 2))
                            v.scalar_tensor_tensor(stage[:, buf], tmp[:], SLOPE, tmp[:], ALU.mult,
                                                   ALU.max).then_inc(s_stage, 1)
                            continue
                        dve.wait_ge(s_zt, cdone(0, i, buf, 2))
                        dve.wait_ge(s_hcopy, cdone(1, i, buf, 2))
                        then(v.scalar_tensor_tensor(z[:, buf], tmp[:], SLOPE, tmp[:], ALU.mult, ALU.max))
                        then(v.tensor_tensor(z[:, buf], z[:, buf], X[:, chunk(i, buf)], ALU.add))
                        layer_norm(z[:, buf], 0, i, buf).then_inc(s_z, 1)
                steps.end(CP, 4 if layer == 0 else 20)

            drop_node, src_all = drop[:, 1:2], src_f
            def last_layer(i):
                for buf in range(2):
                    carry_dst(2, i, buf)
                    dve.wait_ge(s_idx[buf], i * 16 + 16 * (2 * PAIRS + 1))
                    dve.wait_ge(s_srcb, done(0, i, buf, 2))
                    v.tensor_copy(src_f[:, buf], idx[:, buf]).then_inc(s_srcf, 1)
                    dve.wait_ge(s_srcf, done(0, i, buf))
                    dve.wait_ge(s_srcb, done(0, i, buf))
                    dve.wait_ge(s_comb, done(0, i, buf, 1))
                    v.tensor_tensor(equal, ps_gv[:, buf].rearrange("p k (t e) -> p (k t) e", e=P),
                                    along(src_f[:, buf], P), ALU.is_equal).then_inc(s_equal, 1)
                    dve.wait_ge(s_equal, done(0, i, buf))
                    then(v.tensor_tensor(earlier, equal, across(before[:], SLOTS), ALU.mult))
                    then(v.tensor_reduce(dots[:, 6], earlier, AX.X, ALU.add))
                    then(v.tensor_scalar(dots[:, 7], src_f[:, buf], drop_node, None, ALU.subtract))
                    then(v.scalar_tensor_tensor(dots[:, 8], dots[:, 6], 0.0, dots[:, 7], ALU.is_equal, ALU.mult))
                    put_before(dve, i, buf)
                    v.tensor_scalar(put_idx[:, buf], dots[:, 8], drop_node, None, ALU.add).then_inc(s_pidx, 1)
                    dve.wait_ge(s_wc, done(0, i, buf))
                    dve.wait_ge(s_gath[buf], gathered(2, i))
                    then(v.tensor_tensor(prod, G[:, buf], wc[:, buf], ALU.mult))
                    then(v.tensor_reduce(dots[:, 0], by_node(prod), AX.X, ALU.add))
                    dve.wait_ge(s_sq, done(0, i, buf))
                    v.tensor_reduce(dots[:, 1:3].rearrange("p a k -> p (a k)"), by_node(sq), AX.X, ALU.add).then_inc(s_used, 1)
                    dve.wait_ge(s_used, done(0, i, buf))
                    then(v.tensor_tensor(dots[:, 4], dots[:, 1], dots[:, 2], ALU.mult))
                    v.tensor_scalar(dots[:, 3], dots[:, 4], SIM_EPS * SIM_EPS, None, ALU.max).then_inc(s_n2, 1)
                    dve.wait_ge(s_nn, done(0, i, buf))
                    then(v.reciprocal(dots[:, 5], dots[:, 3]))
                    then(v.tensor_tensor(dots[:, 9], dots[:, 0], dots[:, 5], ALU.mult))
                    then(v.tensor_scalar(dots[:, 10], dots[:, 9], 0.0, coef[:, 8:9], ALU.max, ALU.mult))
                    then(v.tensor_scalar(dots[:, 11], dots[:, 9], 0.0, coef[:, 9:10], ALU.min, ALU.mult))
                    then(v.tensor_tensor(dots[:, 10], dots[:, 10], dots[:, 11], ALU.add))
                    then(v.tensor_tensor(dots[:, 9], dots[:, 10], weight[:, ds(i * (2 * SLOTS) + buf * SLOTS, SLOTS)],
                                         ALU.mult))
                    v.tensor_tensor(w_msg, by_node(wc[:, buf]), along(dots[:, 9], D), ALU.mult).then_inc(s_wm, 1)

            steps.begin()
            last_layer(0)
            steps.end()
            with dve.Fori(1, PAIRS) as i:
                steps.begin(i - 1, 26)
                last_layer(i)
            steps.end(PAIRS - 1, 26)

            with dve.Fori(0, CP) as i:
                steps.begin(i, 20)
                for buf in range(2):
                    part = [fin[:, buf, a] for a in range(ACCS)]
                    t = z[:, buf]
                    dve.wait_ge(s_fin[buf], i * (16 * ACCS) + 16 * ACCS)
                    dve.wait_ge(s_out_st[buf], i * 16 + 16)
                    then(v.tensor_tensor(t, part[0], part[1], ALU.add))
                    then(v.tensor_tensor(t, t, part[2], ALU.add))
                    v.tensor_tensor(t, t, part[3], ALU.add).then_inc(s_fused, 1)
                    dve.wait_ge(s_fused, cdone(0, i, buf))
                    then(v.scalar_tensor_tensor(t, X[:, chunk(i, buf)], coef[:, 10:11], t, ALU.mult, ALU.add))
                    then(v.tensor_tensor(t, t, H[:, chunk(i, buf)], ALU.add))
                    layer_norm(t, 1, i, buf).then_inc(s_result, 1)
                steps.end(CP, 20)


_OUT = (N, D)


def kernel(**inputs):
    import concourse.bacc as bacc
    from concourse.bass_utils import run_bass_kernel_spmd

    a = {k: np.asarray(w) for k, w in inputs.items()}

    def edges(w, fill):
        padded = np.full((EP,) + w.shape[1:], fill, w.dtype)
        padded[:E] = w
        return padded

    def by_slot(w):
        return np.ascontiguousarray(w.reshape(2, GROUPS, P, TILES).transpose(2, 1, 3, 0).reshape(P, -1))

    x = np.zeros((NP, D), a["x"].dtype)
    x[:N] = a["x"]
    src, dst = edges(a["src"], 0), edges(a["dst"], N)
    dst_prev = np.concatenate([np.full(1, -1, dst.dtype), dst[:-1]])
    dst_prev[HALF] = -1
    attr = edges(a["edge_attr_32"], 0).reshape(2, GROUPS, COLS, DA).transpose(1, 0, 3, 2)
    arrays = {
        "x": x, "dst_rows": dst.reshape(P, EP // P), "dst_blocks": dst.reshape(SEARCH, SEARCH),
        "dst_prev": dst_prev.reshape(P, EP // P), "block_last": dst.reshape(SEARCH, SEARCH)[:, -1].reshape(1, SEARCH),
        "seam_dst": dst[HALF:HALF + 1].reshape(1, 1), "src_g": by_slot(src), "dst_e": by_slot(dst),
        "adj_e": by_slot(edges(a["edge_weight"], 0)), "deg_e": by_slot(edges(a["edge_weight_n2"], 0)),
        "attr_t": attr.reshape(GROUPS, 2 * DA, COLS),
    }
    for layer in (1, 2):
        for name in ("Wf", "bf", "Ws", "bs", "gw", "gb", "gm"):
            w = a[f"L0_gnn_{name}{layer}"]
            arrays[f"{name}{layer}"] = w if w.ndim == 2 else w.reshape(1, -1)
    arrays["W"] = a["L1_gnn_W"]
    for name in ("b", "deg_coeff", "coeff_param", "scale_param"):
        arrays[name] = a[f"L1_gnn_{name}"].reshape(1, -1)
    arrays = {k: np.ascontiguousarray(w) for k, w in arrays.items()}

    nc = bacc.Bacc("TRN2", target_bir_lowering=False, num_devices=1)
    ap = {k: nc.dram_tensor(f"in_{k}", w.shape, mybir.dt.from_np(w.dtype), kind="ExternalInput").ap()
          for k, w in arrays.items()}
    out = nc.dram_tensor("out", [NP, D], F32, kind="ExternalOutput").ap()
    conv = [[ap[f"{name}{layer}"] for name in ("Wf", "bf", "Ws", "bs", "gw", "gb", "gm")] for layer in (1, 2)]
    gnn(nc, ap["x"], ap["dst_rows"], ap["dst_blocks"], ap["dst_prev"], ap["block_last"], ap["seam_dst"],
        ap["src_g"], ap["src_g"], ap["dst_e"], ap["adj_e"], ap["deg_e"], ap["attr_t"], conv, ap["W"], ap["b"],
        ap["deg_coeff"], ap["coeff_param"], ap["scale_param"], out)
    result = run_bass_kernel_spmd(nc, [{f"in_{k}": w for k, w in arrays.items()}], core_ids=[0])
    return result.results[0]["out"][:N]
```

```python
from contextlib import ExitStack

import numpy as np

import concourse.bass as bass
from concourse import mybir

P = 128
N, E, D, DA = 12500, 200000, 64, 32
TILES = 4
COLS = TILES * P
NT = -(-N // P)
NP = NT * P
GROUPS = 2 * (-(-E // (4 * COLS)))
PAIRS = GROUPS // 2
HALF = GROUPS * COLS
EP = 2 * HALF
SLOTS = 2 * TILES
CH = 7
CHUNKS = NT // CH
CP = CHUNKS // 2
CW = CH * D
SEARCH = 448
SC_COLS = 5
S_COLS = 100
SEARCHES = S_COLS // (2 * SC_COLS)
ACCS = 4
RUNS = SLOTS // ACCS
AROWS = NP + P
PADS_FROM = (N - (P - 1) * NT) * D
ZW = AROWS // P * D // 2
ZI = 49 * D
CLEARS = 2 * ACCS + 1 + EP // P * D // ZI
GATE_MIN = -44.0
EPS = 1e-5
SIM_EPS = 1e-8
SLOPE = 0.01

assert NT % (2 * CH) == 0 and SEARCH * SEARCH == EP and NT + 1 <= S_COLS and N > (P - 1) * NT

ALU = mybir.AluOpType
ACT = mybir.ActivationFunctionType
AX = mybir.AxisListType
F32 = mybir.dt.float32
I32 = mybir.dt.int32
BF16 = mybir.dt.bfloat16
ds = bass.ds


class Steps:

    def __init__(self, engine, sem):
        self.engine, self.sem, self.total, self.k, self.at = engine, sem, 0, 0, 0

    def begin(self, trip=0, per=0):
        self.at, self.k = self.total + trip * per, 0

    def end(self, trips=1, per=None):
        assert per is None or per == self.k, (per, self.k)
        self.total += trips * self.k
        self.at, self.k = self.total, 0

    def then(self, instruction):
        self.k += 1
        instruction.then_inc(self.sem, 1)
        self.engine.wait_ge(self.sem, self.at + self.k)


def gnn(nc, x, dst_rows, dst_blocks, dst_prev, block_last, seam_dst, src_g, src_e, dst_e, adj_e, deg_e,
        attr_t, conv, W, b, deg_coeff, coeff_param, scale_param, out):
    with ExitStack() as ctx:
        def sb(name, shape, dt=F32):
            return ctx.enter_context(nc.sbuf_tensor(name, shape, dt))

        def psum(name, shape):
            return ctx.enter_context(nc.psum_tensor(name, shape, F32))

        def sem(name):
            return ctx.enter_context(nc.semaphore(name))

        def two(name):
            return [sem(f"{name}_{i}") for i in range(2)]

        def dram(name, shape, dt=F32):
            return nc.dram_tensor(name, shape, dt).ap()

        inj_d = dram("first_edge_rows", [EP + P, D])
        sums_d = dram("running_sums", [EP + 1, D])
        same_d = dram("same_dst", [EP], BF16)
        h_d = dram("h_rows", [NP, D])
        wh_d = dram("wh_rows", [NP, D])
        acc_d = [dram(f"by_src_{a}", [AROWS, D]) for a in range(ACCS)]
        inj_groups = inj_d[0:EP].rearrange("(g p r) f -> g p (r f)", p=P, r=SLOTS)
        sums_groups = sums_d[0:EP].rearrange("(g p r) f -> g p (r f)", p=P, r=SLOTS)
        same_groups = same_d.rearrange("(g c) -> g c", c=COLS)

        ident = sb("ident", [P, P])
        ones = sb("ones", [P, P])
        before = sb("before", [P, P])
        zeros = sb("zeros", [P, ZW])
        node_id_i = sb("node_id_i", [P, S_COLS], I32)
        node_id = sb("node_id", [P, S_COLS])
        drop_i = sb("drop_i", [P, 2], I32)
        drop = sb("drop", [P, 2])
        w_dst = sb("w_dst", [P, 2, 2, P])
        w_src = sb("w_src", [P, 2, 2, P])
        w_attr = sb("w_attr", [2 * DA + 1, 2, 2, P])
        norm_w = sb("norm_w", [P, 2, 3, D])
        w_lin = sb("w_lin", [D + 1, D])
        coef_in = sb("coef_in", [P, 6])
        coef = sb("coef", [P, 16])
        last_idx = sb("last_idx", [P, NT])
        first_idx = sb("first_idx", [P, NT])
        seam = sb("seam", [P, NT])
        seam_idx = sb("seam_idx", [P, 1], I32)
        weight = sb("weight", [P, GROUPS * SLOTS])
        H = sb("H", [P, NT * D])
        X = sb("X", [P, NT * D])
        put_nodes = sb("put_nodes", [P, 2, CH], I32)
        get_nodes = sb("get_nodes", [P, 2, CH], I32)
        stage = sb("stage", [P, 2, CW])
        agg = sb("agg", [P, 2, CW])
        z = sb("z", [P, 2, CW])
        tmp = sb("tmp", [P, CW])
        total = sb("total", [P, CW])
        stat = sb("stat", [P, 8, D])
        small = sb("small", [P, 2, 5, CH])
        x2_t = sb("x2_t", [D + 1, 2, CH * P])
        seam_get = sb("seam_get", [P, D])
        seam_row = sb("seam_row", [P, D])
        idx = sb("idx", [P, 2, SLOTS], I32)
        inj = sb("inj", [P, 2, SLOTS * D])
        same = sb("same", [P, 2, COLS], BF16)
        same_sum = sb("same_sum", [P, 2, COLS], BF16)
        attr = sb("attr", [2 * DA + 1, 2, COLS])
        G = sb("G", [P, 2, SLOTS * D])
        xd_t = sb("xd_t", [P, 2, COLS])

        arena = sb("arena", [P, 17600])

        def carve():
            at = [0]

            def tile(*shape, dt=F32):
                n = int(np.prod(shape))
                view = arena[:, at[0]:at[0] + n]
                at[0] += n
                if dt != F32:
                    view = view.bitcast(dt)
                names = "abc"[:len(shape)]
                sizes = dict(zip(names[1:], shape[1:]))
                return view.rearrange(f"p ({' '.join(names)}) -> p {' '.join(names)}", **sizes) if len(shape) > 1 else view
            return tile

        tile = carve()
        dst_now, dst_was, src_i, dst_i = (tile(GROUPS * SLOTS, dt=I32) for _ in range(4))
        deg, deg_tmp = tile(GROUPS * SLOTS), tile(GROUPS * SLOTS)
        last_i, last_f, junk = tile(SEARCH, dt=I32), tile(SEARCH), tile(SEARCH)
        block_rows = tile(2, SC_COLS, SEARCH, dt=I32)
        search = tile(2, 3, SC_COLS)
        block_of, first, valid = tile(S_COLS), tile(S_COLS), tile(NT)
        same_all = sb("same_all", [P, EP // P], BF16)
        block_idx = sb("block_idx", [P, 2, SC_COLS], I32)

        tile = carve()
        squares = tile(NT * D)
        xs_t = tile(2, COLS)
        gv = tile(2, 2, COLS)
        soft, msg = tile(COLS), tile(COLS)
        sum_t = tile(2, COLS)
        sums = tile(2, SLOTS * D)

        tile = carve()
        wc = tile(2, SLOTS * D)
        prod = tile(SLOTS * D)
        sq = tile(2 * SLOTS * D)
        dots = tile(12, SLOTS)
        src_f = tile(2, SLOTS)
        equal = tile(2, SLOTS * P)
        earlier = tile(SLOTS, P)
        w_msg = tile(2, SLOTS * D)
        put = tile(2, SLOTS * D)
        fin = tile(2, ACCS, CW)
        put_idx = sb("put_idx", [P, 2, SLOTS], I32)

        ps_inj = psum("ps_inj", [P, COLS])
        ps_g = psum("ps_g", [P, COLS])
        ps_gv = psum("ps_gv", [P, 2, 2, COLS])
        ps_out = psum("ps_out", [P, COLS])

        s_nodes = sem("x_loaded")
        s_search = sem("search_inputs_loaded")
        s_edges = sem("edge_scalars_loaded")
        s_weights = sem("weights_loaded")
        s_zeros = sem("zeros_set")
        s_tiles = sem("weight_tiles_zeroed")
        s_pool = sem("pool_constants")
        s_cleared = sem("tables_cleared")
        s_same_set = sem("same_set")
        s_same = sem("same_stored")
        s_dve = sem("dve_steps")
        s_act = sem("act_steps")
        s_ptick = sem("pool_waited")
        s_atick = sem("act_waited")
        s_petick = sem("pe_waited")
        s_bidx = sem("block_idx_ready")
        s_rows = two("block_rows_gathered")
        s_deg = sem("deg_ready")
        s_dega = sem("deg_activated")
        s_setup = sem("setup_done")
        s_pnodes = sem("put_nodes_ready")
        s_stage = sem("stage_ready")
        s_scat = sem("node_columns_scattered")
        s_table = two("chunk_stored")
        s_gnodes = sem("get_nodes_ready")
        s_agg = two("agg_gathered")
        s_part = sem("partition_sums")
        s_tot = sem("node_sums")
        s_var = sem("variance_ready")
        s_std = sem("std_ready")
        s_hcopy = sem("h_copied")
        s_seam = sem("seam_sums_loaded")
        s_sget = sem("seam_row_gathered")
        s_sput = sem("seam_row_put")
        s_pads = sem("padded_nodes_zeroed")
        s_lnv = sem("ln_variance_ready")
        s_lnr = sem("ln_root_ready")
        s_z = sem("x2_ready")
        s_zt = sem("x2_turned")
        s_ztc = sem("x2_turned_copied")
        s_wh = sem("wh_ready")
        s_whc = sem("wh_copied")
        s_fin = two("by_src_loaded")
        s_fused = sem("by_src_used")
        s_result = sem("result_ready")
        s_out_st = two("result_stored")
        s_idx = two("idx_loaded")
        s_load = two("group_loaded")
        s_attr = two("attr_loaded")
        s_same_sum = two("same_loaded_again")
        s_gath = two("src_rows_gathered")
        s_injt = sem("inj_turned")
        s_scan = sem("dst_rows_carried")
        s_gt = sem("src_rows_turned")
        s_xs = sem("src_rows_copied")
        s_gates = sem("gates_ready")
        s_fold = sem("gates_clamped")
        s_soft = sem("softplus_ready")
        s_lns = sem("gates_activated")
        s_msg = sem("messages_ready")
        s_sumt = sem("messages_summed")
        s_turned = sem("sums_turned")
        s_sums = sem("sums_copied")
        s_stored = two("sums_stored")
        s_wt = sem("wc_turned")
        s_wc = sem("wc_copied")
        s_sq = sem("squares_ready")
        s_n2 = sem("norm_products_ready")
        s_nn = sem("norm_product_roots")
        s_used = sem("src_rows_used")
        s_srcf = sem("src_float")
        s_srcb = sem("src_spread")
        s_equal = sem("equal_ready")
        s_pidx = sem("put_idx_ready")
        s_wm = sem("weighted_ready")
        s_comb = sem("combined")
        s_put = sem("put_ready")
        s_added = two("added")

        by_two = [s_bidx, s_pnodes, s_stage, s_gnodes, s_hcopy, s_lnv, s_lnr, s_z, s_zt, s_ztc, s_wh, s_whc,
                  s_fused, s_result, s_injt, s_scan, s_gt, s_xs, s_gates, s_fold, s_soft, s_lns, s_msg,
                  s_sumt, s_turned, s_sums, s_wt, s_wc, s_sq, s_n2, s_nn, s_used, s_srcf, s_srcb,
                  s_equal, s_pidx, s_wm, s_comb, s_put]
        by_sp = [s_table, s_out_st, s_stored]

        def done(rnd, h, buf, back=0):
            return h * 2 + (rnd * GROUPS + buf + 3 - back)

        def cdone(rnd, h, buf, back=0):
            return h * 2 + (rnd * CHUNKS + buf + 3 - back)

        def scattered(rnd, h, buf, column=CH):
            return h * (32 * CH) + 16 * (rnd * NT + buf * CH + column)

        def tabled(rnd, h, back=0):
            return h * 16 + 16 * (rnd * CP + 2 - back)

        def stored(rnd, h, back=0):
            return h * 16 + 16 * (rnd * PAIRS + 2 - back)

        def loaded(layer, h):
            return h * 48 + 48 * (layer * PAIRS + 1)

        def loaded_one(amount, layer, h):
            return h * amount + amount * (layer * PAIRS + 1)

        def gathered(layer, h):
            return h * (16 * SLOTS) + 16 * SLOTS * (layer * PAIRS + 1)

        def added(h, buf, run):
            return h * (16 * SLOTS) + 16 * (buf * SLOTS + run * ACCS) // 2

        def put_before(engine, h, buf):
            for half in range(2):
                if not at_start(h):
                    engine.wait_ge(s_added[half], added(h, buf, 0) - 8 * SLOTS)

        def at_start(h):
            return isinstance(h, int) and h == 0

        def all_trips(engine, body, trips):
            body(0)
            with engine.Fori(1, trips) as i:
                body(i)

        def chunk(h, buf):
            return ds(h * (2 * CW) + buf * CW, CW)

        def ccols(h, buf):
            return ds(h * (2 * CH) + buf * CH, CH)

        def nodes(ap):
            return ap.rearrange("(p t) f -> p (t f)", p=P)

        def by_node(ap):
            return ap.rearrange("p (c f) -> p c f", f=D)

        def across(ap, n):
            return ap.unsqueeze(1).to_broadcast([P, n, ap.shape[1]])

        def along(ap, n):
            return ap.unsqueeze(2).to_broadcast([P, ap.shape[1], n])

        def turned(ap, j):
            return ap.rearrange("p (q j) -> p q j", j=TILES)[:, :, j]

        def pipeline(engine, *stages, steps=None, per=0):
            def step(i, buf):
                for stage_, lag in stages:
                    h = i + (buf - lag) // 2
                    if not isinstance(h, int) or 0 <= h < PAIRS:
                        stage_(h, (buf - lag) % 2)

            lags = [lag for _, lag in stages]
            head, tail = max(1, -(-max(lags) // 2)), PAIRS - -(min(lags) // 2)
            if steps:
                steps.begin()
            for k in range(2 * head):
                step(k // 2, k % 2)
            if steps:
                steps.end()
            with engine.Fori(head, tail) as i:
                if steps:
                    steps.begin(i - head, per)
                step(i, 0)
                step(i, 1)
            if steps:
                steps.end(tail - head, per)
                steps.begin()
            for k in range(2 * tail, GROUPS + max(lags)):
                step(k // 2, k % 2)
            if steps:
                steps.end()

        block = ctx.enter_context(nc.Block())

        @block.sync
        def _(sp):
            def load(out_, in_, s):
                sp.dma_start(out_, in_).then_inc(s, 16)

            load(last_i, block_last.to_broadcast([P, SEARCH]), s_search)
            load(dst_now, dst_rows, s_search)
            load(dst_was, dst_prev, s_search)
            load(X[:], nodes(x), s_nodes)
            load(H[:], nodes(x), s_nodes)
            load(dst_i, dst_e, s_edges)
            load(src_i, src_e, s_edges)
            load(weight[:], adj_e, s_edges)
            load(deg, deg_e, s_edges)
            load(seam_idx[:], seam_dst.to_broadcast([P, 1]), s_edges)
            load(coef_in[:, 0:2], deg_coeff.to_broadcast([P, 2]), s_edges)
            load(coef_in[:, 2:5], coeff_param.to_broadcast([P, 3]), s_edges)
            load(coef_in[:, 5:6], scale_param.to_broadcast([P, 1]), s_edges)
            sp.wait_ge(s_same_set, 1)
            load(same_d.rearrange("(p c) -> p c", p=P), same_all[:], s_same)
            sp.wait_ge(s_tiles, 1)
            for layer, (Wf, bf, Ws, bs, gw, gb, gm) in enumerate(conv):
                for k, (w, bias) in enumerate(((Wf, bf), (Ws, bs))):
                    for s in range(2):
                        o = slice(s * D, (s + 1) * D)
                        load(w_dst[o, layer, k, o], w[0:D, :], s_weights)
                        load(w_src[o, layer, k, o], w[D:2 * D, :], s_weights)
                        load(w_attr[s * DA:(s + 1) * DA, layer, k, o], w[2 * D:, :], s_weights)
                        load(w_attr[2 * DA:2 * DA + 1, layer, k, o], bias, s_weights)
                for k, v in enumerate((gw, gb, gm)):
                    load(norm_w[:, layer, k, :], v.to_broadcast([P, D]), s_weights)
            load(w_lin[0:D, :], W, s_weights)
            load(w_lin[D:D + 1, :], b, s_weights)
            sp.wait_ge(s_same, 16)

            for layer in range(3):
                sp.wait_ge(s_scat, 16 * NT * (layer + 1))
                sp.wait_ge(s_sget, 16 * (layer + 1))
                load(inj_d[1:2, :], seam_get[0:1, :], s_sput)
                sp.wait_ge(s_sput, 16 * (layer + 1))

                def load_idx(h, buf):
                    if not at_start(h):
                        if layer < 2:
                            sp.wait_ge(s_gath[buf], gathered(layer, h - 1))
                        else:
                            sp.wait_ge(s_used, done(0, h, buf, 2))
                    load(idx[:, buf], src_g[:, ds((h * 2 + buf) * SLOTS, SLOTS)], s_idx[buf])

                def load_group(h, buf):
                    g = h * 2 + buf
                    sp.wait_ge(s_scan, done(layer, h, buf, 2))
                    load(inj[:, buf], inj_groups[ds(g, 1)].rearrange("a p c -> p (a c)"), s_load[buf])
                    load_same(same, s_load, g, buf)
                    if layer < 2:
                        sp.wait_ge(s_gates, done(layer, h, buf, 2))
                        load(attr[0:2 * DA, buf], attr_t[ds(g, 1)].rearrange("a k c -> k (a c)"), s_attr[buf])

                def load_same(tile_, s, g, buf):
                    for half in range(2):
                        load(tile_[half * D:(half + 1) * D, buf],
                             same_groups[ds(g + half * GROUPS, 1), :].to_broadcast([D, COLS]), s[buf])

                def load_again(h, buf):
                    sp.wait_ge(s_sumt, done(layer, h, buf, 2))
                    load_same(same_sum, s_same_sum, h * 2 + buf, buf)

                def store_sums(h, buf):
                    g = h * 2 + buf
                    sp.wait_ge(s_sums, done(layer, h, buf))
                    load(sums_groups[ds(g, 1)].rearrange("a p c -> p (a c)"), sums[:, buf], s_stored[buf])

                if layer == 2:
                    load_idx(0, 0)
                    load_idx(0, 1)
                    pipeline(sp, (load_group, 0), (load_idx, -2))
                    break
                load_idx(0, 0)
                load_idx(0, 1)
                pipeline(sp, (load_group, 0), (load_idx, -2), (load_again, 1), (store_sums, 3))
                for buf in range(2):
                    sp.wait_ge(s_stored[buf], stored(layer, PAIRS - 1))
                load(seam_row[:], sums_d[EP - 2:EP - 1, :].to_broadcast([P, D]), s_seam)
                table_out = nodes((h_d, wh_d)[layer])
                with sp.Fori(0, CP) as i:
                    for buf in range(2):
                        sp.wait_ge(s_stage, cdone(layer + 1, i, buf))
                        load(table_out[:, chunk(i, buf)], stage[:, buf], s_table[buf])
                if layer == 0:
                    sp.wait_ge(s_hcopy, cdone(0, CP - 1, 1))
                    load(H[P - 1:P, PADS_FROM:NT * D], zeros[0:1, 0:NT * D - PADS_FROM], s_pads)

            for half in range(2):
                sp.wait_ge(s_added[half], 8 * GROUPS * SLOTS)
            with sp.Fori(0, CP) as i:
                for buf in range(2):
                    sp.wait_ge(s_fused, cdone(0, i, buf, 2))
                    for a in range(ACCS):
                        load(fin[:, buf, a], nodes(acc_d[a][0:NP])[:, chunk(i, buf)], s_fin[buf])
                for buf in range(2):
                    sp.wait_ge(s_result, cdone(0, i, buf))
                    load(nodes(out)[:, chunk(i, buf)], z[:, buf], s_out_st[buf])
            for buf in range(2):
                sp.wait_ge(s_out_st[buf], 16 * (CP + 1))

        @block.gpsimd
        def _(pool):
            pool.memset(ident[:], 0.0).then_inc(s_pool, 1)
            pool.memset(before[:], 1.0).then_inc(s_pool, 1)
            pool.wait_ge(s_pool, 2)
            pool.affine_select(out=ident[:], in_=ident[:], compare_op=ALU.not_equal, fill=1.0, base=0,
                               pattern=[[-1, P]], channel_multiplier=1).then_inc(s_pool, 1)
            pool.affine_select(out=before[:], in_=before[:], compare_op=ALU.is_gt, fill=0.0, base=0,
                               pattern=[[-1, P]], channel_multiplier=1).then_inc(s_pool, 1)
            pool.iota(node_id_i[:], pattern=[[1, S_COLS]], base=0, channel_multiplier=NT).then_inc(s_pool, 1)
            pool.iota(drop_i[:, 0:1], pattern=[[1, 1]], base=EP, channel_multiplier=1).then_inc(s_pool, 1)
            pool.iota(drop_i[:, 1:2], pattern=[[1, 1]], base=NP, channel_multiplier=1).then_inc(s_pool, 1)

            def wait(s, value):
                pool.wait_ge(s, value)
                pool.sem_inc(s_ptick, 1)

            def gather(out_, table_in, index, s):
                pool.indirect_dma_start(out_, None, table_in, bass.IndirectOffsetOnAxis(ap=index, axis=0)).then_inc(s, 16)

            with pool.Fori(0, SEARCHES) as i:
                for buf in range(2):
                    wait(s_bidx, cdone(0, i, buf))
                    for c in range(SC_COLS):
                        gather(block_rows[:, buf, c], dst_blocks, block_idx[:, buf, c:c + 1], s_rows[buf])

            for layer in range(3):
                if layer == 0:
                    pool.wait_ge(s_cleared, 16 * CLEARS)
                def put_rows(h):
                    for buf in range(2):
                        wait(s_pnodes, cdone(layer, h, buf))
                        wait(s_stage, cdone(layer, h, buf))
                        for c in range(CH):
                            if layer or buf or c or not at_start(h):
                                wait(s_scat, scattered(layer, h, buf, c))
                            pool.indirect_dma_start(
                                inj_d, bass.IndirectOffsetOnAxis(ap=put_nodes[:, buf, c:c + 1], axis=0),
                                stage[:, buf, c * D:(c + 1) * D], None).then_inc(s_scat, 16)

                all_trips(pool, put_rows, CP)
                table_in = (x, h_d, wh_d)[layer]
                if layer:
                    for buf in range(2):
                        pool.wait_ge(s_table[buf], tabled(layer - 1, CP - 1))
                else:
                    pool.wait_ge(s_edges, 16 * 8)
                if layer:
                    pool.wait_ge(s_sput, 16 * layer)
                gather(seam_get[:], table_in, seam_idx[:], s_sget)

                def gather_group(h, buf, first=0, to=SLOTS):
                    if first == 0:
                        wait(s_idx[buf], h * 16 + 16 * (layer * PAIRS + 1))
                        if layer < 2:
                            wait(s_gt, done(layer, h, buf, 2))
                        else:
                            wait(s_used, done(0, h, buf, 2))
                    for k in range(first, to):
                        gather(G[:, buf, k * D:(k + 1) * D], table_in, idx[:, buf, k:k + 1], s_gath[buf])

                def add_run(h, buf, run):
                    if run == 0:
                        wait(s_pidx, done(0, h, buf))
                        wait(s_put, done(0, h, buf))
                    for a in range(ACCS):
                        half = a // (ACCS // 2)
                        if a % (ACCS // 2) == 0 and (run or buf or not at_start(h)):
                            wait(s_added[half], added(h, buf, run))
                        k = run * ACCS + a
                        pool.indirect_dma_start(
                            acc_d[a], bass.IndirectOffsetOnAxis(ap=put_idx[:, buf, k:k + 1], axis=0),
                            put[:, buf, k * D:(k + 1) * D], None, compute_op=ALU.add).then_inc(s_added[half], 16)

                if layer == 2:
                    split = SLOTS - ACCS // 2
                    pipeline(pool, (lambda h, buf: gather_group(h, buf, 0, split), 0),
                             (lambda h, buf: add_run(h, buf, 0), 2),
                             (lambda h, buf: gather_group(h, buf, split, SLOTS), 0),
                             (lambda h, buf: add_run(h, buf, 1), 2))
                    break
                with pool.Fori(0, PAIRS) as i:
                    for buf in range(2):
                        gather_group(i, buf)
                for buf in range(2):
                    pool.wait_ge(s_stored[buf], stored(layer, PAIRS - 1))
                with pool.Fori(0, CP) as i:
                    for buf in range(2):
                        wait(s_gnodes, cdone(layer, i, buf))
                        for c in range(CH):
                            gather(agg[:, buf, c * D:(c + 1) * D], sums_d, get_nodes[:, buf, c:c + 1], s_agg[buf])

        @block.tensor
        def _(pe):
            pe.wait_ge(s_pool, 7)
            pe.wait_ge(s_weights, 16 * (2 * 19 + 2))

            def turn_inj(layer, h, buf):
                pe.wait_ge(s_load[buf], loaded(layer, h))
                pe.wait_ge(s_scan, done(layer, h, buf, 1))
                for j in range(TILES):
                    mm = pe.transpose(turned(ps_inj, j), inj[:, buf, j * P:(j + 1) * P], ident[:])
                mm.then_inc(s_injt, 1)

            for layer in range(2):
                def turn_rows(h, buf):
                    turn_inj(layer, h, buf)
                    pe.wait_ge(s_gath[buf], gathered(layer, h))
                    pe.wait_ge(s_xs, done(layer, h, buf, 1))
                    for j in range(TILES):
                        mm = pe.transpose(turned(ps_g, j), G[:, buf, j * P:(j + 1) * P], ident[:])
                    mm.then_inc(s_gt, 1)

                def products(h, buf):
                    pe.wait_ge(s_soft, done(layer, h, buf, 2))
                    pe.wait_ge(s_attr[buf], loaded_one(16, layer, h))
                    for k in range(2):
                        pe.matmul(ps_gv[:, buf, k], w_attr[:, layer, k], attr[:, buf], start=True, stop=False)
                    pe.wait_ge(s_xs, done(layer, h, buf))
                    for k in range(2):
                        pe.matmul(ps_gv[:, buf, k], w_src[:, layer, k], xs_t[:, buf], start=False, stop=False)
                    pe.wait_ge(s_scan, done(layer, h, buf))
                    for k in range(2):
                        mm = pe.matmul(ps_gv[:, buf, k], w_dst[:, layer, k], xd_t[:, buf], start=False, stop=True)
                    mm.then_inc(s_gates, 1)

                def turn_sums(h, buf):
                    pe.wait_ge(s_sumt, done(layer, h, buf))
                    pe.wait_ge(s_sums, done(layer, h, buf, 1))
                    for j in range(TILES):
                        mm = pe.transpose(ps_out[:, j * P:(j + 1) * P], turned(sum_t[:, buf], j), ident[:])
                    mm.then_inc(s_turned, 1)

                pipeline(pe, (turn_rows, 0), (products, 1), (turn_sums, 2))
                pe.wait_ge(s_part, 2 * layer + 1)
                pe.matmul(ps_out[:, 0:CW], ones[:], total[:], start=True, stop=True).then_inc(s_tot, 1)
                pe.wait_ge(s_part, 2 * layer + 2)
                pe.matmul(ps_out[:, 0:D], ones[:], stat[:, 2], start=True, stop=True).then_inc(s_tot, 1)

            with pe.Fori(0, CP) as i:
                for buf in range(2):
                    pe.wait_ge(s_z, cdone(0, i, buf))
                    pe.wait_ge(s_ztc, cdone(0, i, buf, 1))
                    pe.sem_inc(s_petick, 1)
                    for c in range(CH):
                        mm = pe.transpose(ps_gv[0:D, 0, c // TILES, c % TILES * P:(c % TILES + 1) * P],
                                          z[:, buf, c * D:(c + 1) * D], ident[:])
                    mm.then_inc(s_zt, 1)
                    pe.wait_ge(s_ztc, cdone(0, i, buf))
                    pe.wait_ge(s_whc, cdone(0, i, buf, 1))
                    for c in range(CH):
                        mm = pe.matmul(ps_out[:, c * D:(c + 1) * D], x2_t[:, buf, c * P:(c + 1) * P], w_lin[:],
                                       start=True, stop=True)
                    mm.then_inc(s_wh, 1)

            spread = ps_gv.rearrange("p b k (t e) -> p b (k t) e", e=P)

            def turn_src_dst(h, buf):
                turn_inj(2, h, buf)
                pe.wait_ge(s_srcf, done(0, h, buf))
                pe.wait_ge(s_equal, done(0, h, buf, 2))
                for k in range(SLOTS):
                    mm = pe.transpose(spread[:, buf, k], src_f[:, buf, k:k + 1].to_broadcast([P, P]), ident[:])
                mm.then_inc(s_srcb, 1)
                pe.wait_ge(s_scan, done(2, h, buf))
                pe.wait_ge(s_sq, done(0, h, buf, 1))
                for j in range(TILES):
                    mm = pe.transpose(ps_g[:, j * P:(j + 1) * P], turned(xd_t[:, buf], j), ident[:])
                mm.then_inc(s_wt, 1)

            def combine(h, buf):
                pe.wait_ge(s_equal, done(0, h, buf))
                pe.wait_ge(s_wm, done(0, h, buf))
                pe.wait_ge(s_put, done(0, h, buf, 1))
                for k in range(SLOTS):
                    mm = pe.matmul(ps_out[:, k * D:(k + 1) * D], equal[:, buf, k * P:(k + 1) * P],
                                   w_msg[:, buf, k * D:(k + 1) * D], start=True, stop=True)
                mm.then_inc(s_comb, 1)

            pipeline(pe, (turn_src_dst, 0), (combine, 1))

        @block.scalar
        def _(act):
            steps = Steps(act, s_act)
            act.wait_ge(s_zeros, 1)
            for a in range(ACCS):
                rows_a = acc_d[a].rearrange("(p r) f -> p (r f)", p=P)
                for k in range(2):
                    act.dma_start(rows_a[:, k * ZW:(k + 1) * ZW], zeros[:]).then_inc(s_cleared, 16)
            act.dma_start(sums_d[EP:EP + 1, :], zeros[0:1, 0:D]).then_inc(s_cleared, 16)
            inj_rows = inj_d[0:EP].rearrange("(p r) f -> p (r f)", p=P)
            with act.Fori(0, EP // P * D // ZI) as i:
                act.dma_start(inj_rows[:, ds(i * ZI, ZI)], zeros[:, 0:ZI]).then_inc(s_cleared, 16)

            def wait(s, value):
                act.wait_ge(s, value)
                act.sem_inc(s_atick, 1)

            act.wait_ge(s_deg, 1)
            steps.begin()
            steps.then(nc.scalar.activation(deg_tmp, deg_tmp, ACT.Exp))
            steps.then(nc.scalar.activation(coef[:, 0:4], coef[:, 0:4], ACT.Exp))
            steps.then(nc.scalar.activation(coef[:, 3:4], coef[:, 3:4], ACT.Ln, bias=1.0))
            nc.scalar.activation(deg_tmp, deg_tmp, ACT.Ln, bias=1.0).then_inc(s_dega, 1)
            steps.end()

            act.wait_ge(s_setup, 1)
            for layer in range(2):
                def copy_rows(h, buf):
                    act.wait_ge(s_gt, done(layer, h, buf))
                    act.wait_ge(s_gates, done(layer, h, buf, 2))
                    nc.scalar.copy(xs_t[:, buf], ps_g[:]).then_inc(s_xs, 1)

                def gates(h, buf):
                    act.wait_ge(s_gates, done(layer, h, buf))
                    act.wait_ge(s_msg, done(layer, h, buf, 2))
                    steps.then(nc.scalar.activation(gv[:, buf, 1], ps_gv[:, buf, 1], ACT.Abs))
                    act.wait_ge(s_fold, done(layer, h, buf))
                    both = gv[:, buf].rearrange("p k c -> p (k c)")
                    steps.then(nc.scalar.activation(both, both, ACT.Exp, scale=-1.0))
                    steps.then(nc.scalar.activation(both, both, ACT.Ln, bias=1.0))
                    nc.scalar.activation(both[:, 0:COLS], both[:, 0:COLS], ACT.Exp, scale=-1.0).then_inc(s_lns, 1)

                def copy_sums(h, buf):
                    act.wait_ge(s_turned, done(layer, h, buf))
                    act.wait_ge(s_stored[buf], stored(layer, h, 1))
                    nc.scalar.copy(sums[:, buf], ps_out[:]).then_inc(s_sums, 1)

                nc.scalar.preload_act_table_set("natural_log_exp_and_others")
                pipeline(act, (copy_rows, 0), (gates, 1), (copy_sums, 2), steps=steps, per=6)

                act.wait_ge(s_var, layer + 1)
                nc.scalar.activation(stat[:, 4], stat[:, 4], ACT.Sqrt).then_inc(s_std, 1)
                if layer == 0:
                    with act.Fori(0, CP) as i:
                        for buf in range(2):
                            wait(s_stage, cdone(1, i, buf))
                            nc.scalar.copy(H[:, chunk(i, buf)], stage[:, buf]).then_inc(s_hcopy, 1)
                    continue
                with act.Fori(0, CP) as i:
                    for buf in range(2):
                        act.wait_ge(s_lnv, cdone(0, i, buf))
                        nc.scalar.activation(small[:, buf, 2], small[:, buf, 2], ACT.Sqrt).then_inc(s_lnr, 1)
                        wait(s_z, cdone(0, i, buf))
                        nc.scalar.copy(H[:, chunk(i, buf)], z[:, buf]).then_inc(s_hcopy, 1)
                        act.wait_ge(s_zt, cdone(0, i, buf))
                        act.wait_ge(s_wh, cdone(0, i, buf, 2))
                        for k, n in ((0, TILES * P), (1, (CH - TILES) * P)):
                            c = nc.scalar.copy(x2_t[0:D, buf, k * COLS:k * COLS + n], ps_gv[0:D, 0, k, 0:n])
                        c.then_inc(s_ztc, 1)
                        act.wait_ge(s_wh, cdone(0, i, buf))
                        act.wait_ge(s_scat, scattered(2, i, buf - 2))
                        act.wait_ge(s_table[buf], tabled(1, i, 1))
                        nc.scalar.copy(stage[:, buf], ps_out[:, 0:CW]).then_inc(s_stage, 1)
                        nc.scalar.copy(X[:, chunk(i, buf)], ps_out[:, 0:CW]).then_inc(s_whc, 1)

            def dst_rows(h, buf):
                act.wait_ge(s_wt, done(0, h, buf))
                act.wait_ge(s_wm, done(0, h, buf, 2))
                nc.scalar.copy(wc[:, buf], ps_g[:]).then_inc(s_wc, 1)
                act.wait_ge(s_n2, done(0, h, buf, 1))
                nc.scalar.activation(sq[:, 0:SLOTS * D], ps_g[:], ACT.Square)

            def copy_put(h, buf):
                act.wait_ge(s_comb, done(0, h, buf))
                put_before(act, h, buf)
                nc.scalar.copy(put[:, buf], ps_out[:]).then_inc(s_put, 1)

            def src_squares(h, buf):
                act.wait_ge(s_gath[buf], gathered(2, h))
                nc.scalar.activation(sq[:, SLOTS * D:], G[:, buf], ACT.Square).then_inc(s_sq, 1)
                act.wait_ge(s_n2, done(0, h, buf))
                nc.scalar.activation(dots[:, 3], dots[:, 3], ACT.Sqrt).then_inc(s_nn, 1)

            pipeline(act, (dst_rows, 0), (copy_put, 1), (src_squares, 0))

            with act.Fori(0, CP) as i:
                for buf in range(2):
                    act.wait_ge(s_lnv, cdone(1, i, buf))
                    nc.scalar.activation(small[:, buf, 2], small[:, buf, 2], ACT.Sqrt).then_inc(s_lnr, 1)

        @block.vector
        def _(dve):
            v = nc.vector
            steps = Steps(dve, s_dve)
            then = steps.then
            v.memset(zeros[:], 0.0).then_inc(s_zeros, 1)
            for s in by_two:
                dve.sem_inc(s, 2)
            for pair in by_sp:
                for s in pair:
                    dve.sem_inc(s, 16)
            for t in (w_dst, w_src):
                v.memset(t[:], 0.0)
            v.memset(w_attr[:], 0.0).then_inc(s_tiles, 1)
            v.memset(ones[:], 1.0)
            v.memset(attr[2 * DA:2 * DA + 1], 1.0)
            v.memset(x2_t[D:D + 1], 1.0)
            steps.begin()
            then(v.memset(xd_t[:, 1, COLS - 1:COLS], 0.0))
            dve.wait_ge(s_search, 48)
            v.tensor_tensor(same_all[:], dst_now, dst_was, ALU.is_equal).then_inc(s_same_set, 1)
            then(v.tensor_copy(last_f, last_i))
            dve.wait_ge(s_pool, 7)
            then(v.tensor_copy(node_id[:], node_id_i[:]))
            then(v.tensor_copy(drop[:], drop_i[:]))
            steps.end()


            def find_block(h, buf):
                at = ds(h * (2 * SC_COLS) + buf * SC_COLS, SC_COLS)
                then(v.tensor_scalar(search[:, buf, 0], node_id[:, at], 0.0, None, ALU.add))
                for c in range(SC_COLS):
                    then(v.tensor_scalar(junk, last_f, search[:, buf, 0, c:c + 1], 0.0, ALU.is_lt, ALU.add,
                                         accum_out=search[:, buf, 1, c:c + 1]))
                then(v.tensor_scalar(search[:, buf, 2], search[:, buf, 1], float(SEARCH - 1), None, ALU.min))
                v.tensor_scalar(block_idx[:, buf], search[:, buf, 2], 0.0, None, ALU.add).then_inc(s_bidx, 1)

            def find_edge(h, buf):
                dve.wait_ge(s_rows[buf], h * (16 * SC_COLS) + 16 * SC_COLS)
                for c in range(SC_COLS):
                    then(v.tensor_scalar(junk, block_rows[:, buf, c], search[:, buf, 0, c:c + 1], 0.0, ALU.is_lt,
                                         ALU.add, accum_out=search[:, buf, 1, c:c + 1]))
                then(v.scalar_tensor_tensor(first[:, ds(h * (2 * SC_COLS) + buf * SC_COLS, SC_COLS)], search[:, buf, 2],
                                            float(SEARCH), search[:, buf, 1], ALU.mult, ALU.add))

            def lagged(now, later, trips, per):
                steps.begin()
                now(0, 0)
                steps.end()
                with dve.Fori(0, trips - 1) as i:
                    steps.begin(i, per)
                    now(i, 1)
                    later(i, 0)
                    now(i + 1, 0)
                    later(i, 1)
                steps.end(trips - 1, per)
                steps.begin()
                now(trips - 1, 1)
                later(trips - 1, 0)
                later(trips - 1, 1)
                steps.end()

            lagged(find_block, find_edge, SEARCHES, 26)

            steps.begin()
            f, e = first[:, 0:NT], first[:, 1:NT + 1]
            then(v.tensor_tensor(valid, e, f, ALU.is_gt))
            then(v.scalar_tensor_tensor(valid, node_id[:, 0:NT], float(N), valid, ALU.is_lt, ALU.mult))
            row = squares[:, 0:NT]
            then(v.tensor_scalar(row, f, float(HALF), float(EP - 1), ALU.is_ge, ALU.mult))
            then(v.scalar_tensor_tensor(row, f, 2.0, row, ALU.mult, ALU.subtract))
            then(v.scalar_tensor_tensor(first_idx[:], row, drop[:, 0:1], valid, ALU.subtract, ALU.mult))
            then(v.tensor_scalar(first_idx[:], first_idx[:], drop[:, 0:1], None, ALU.add))
            then(v.tensor_scalar(row, e, float(HALF), float(EP - 1), ALU.is_gt, ALU.mult))
            then(v.scalar_tensor_tensor(row, e, 2.0, row, ALU.mult, ALU.subtract))
            then(v.scalar_tensor_tensor(last_idx[:], row, float(EP + 2), valid, ALU.subtract, ALU.mult))
            then(v.tensor_scalar(last_idx[:], last_idx[:], float(EP), None, ALU.add))
            then(v.tensor_scalar(seam[:], f, float(HALF), None, ALU.is_lt))
            then(v.scalar_tensor_tensor(seam[:], e, float(HALF), seam[:], ALU.is_gt, ALU.mult))

            dve.wait_ge(s_edges, 16 * 8)
            then(v.tensor_scalar(deg, deg, coef_in[:, 0:1], coef_in[:, 1:2], ALU.mult, ALU.add))
            then(v.scalar_tensor_tensor(deg_tmp, deg, -1.0, deg, ALU.mult, ALU.min))
            then(v.tensor_reduce(coef[:, 4:5], coef_in[:, 2:5], AX.X, ALU.max))
            then(v.tensor_scalar(coef[:, 0:3], coef_in[:, 2:5], coef[:, 4:5], None, ALU.subtract))
            v.scalar_tensor_tensor(coef[:, 3:4], coef_in[:, 5:6], -1.0, coef_in[:, 5:6], ALU.mult,
                                   ALU.min).then_inc(s_deg, 1)
            steps.end()

            dve.wait_ge(s_nodes, 32)

            def stage_idx(rnd, h, buf):
                if rnd or not at_start(h):
                    dve.wait_ge(s_scat, scattered(rnd, h, buf - 2))
                v.tensor_scalar(put_nodes[:, buf], first_idx[:, ccols(h, buf)], 0.0, None,
                                ALU.add).then_inc(s_pnodes, 1)

            def stage_x(h):
                for buf in range(2):
                    stage_idx(0, h, buf)
                    v.tensor_scalar(stage[:, buf], X[:, chunk(h, buf)], 1.0, None, ALU.mult).then_inc(s_stage, 1)

            all_trips(dve, stage_x, CP)

            steps.begin()
            dve.wait_ge(s_dega, 1)
            then(v.scalar_tensor_tensor(deg, deg, 0.0, deg_tmp, ALU.max, ALU.add))
            then(v.tensor_tensor(deg_tmp, src_i, dst_i, ALU.not_equal))
            then(v.tensor_tensor(weight[:], weight[:], deg, ALU.mult))
            then(v.tensor_tensor(weight[:], weight[:], deg_tmp, ALU.mult))
            then(v.scalar_tensor_tensor(coef[:, 5:6], coef_in[:, 5:6], 0.0, coef[:, 3:4], ALU.max, ALU.add))
            then(v.tensor_reduce(coef[:, 6:7], coef[:, 0:3], AX.X, ALU.add))
            then(v.reciprocal(coef[:, 7:8], coef[:, 6:7]))
            then(v.tensor_tensor(coef[:, 7:8], coef[:, 7:8], coef[:, 5:6], ALU.mult))
            then(v.tensor_scalar(coef[:, 8:11], coef[:, 0:3], coef[:, 7:8], None, ALU.mult))
            then(v.memset(sum_t[:, 1, COLS - 1:COLS], 0.0))
            dve.sem_inc(s_setup, 1)
            steps.end()

            def carry_dst(layer, h, buf):
                dve.wait_ge(s_injt, done(layer, h, buf))
                dve.wait_ge(s_load[buf], loaded(layer, h))
                if layer < 2:
                    dve.wait_ge(s_gates, done(layer, h, buf, 2))
                else:
                    dve.wait_ge(s_wt, done(0, h, buf, 2))
                dve.wait_ge(s_scan, done(layer, h, buf, 1))
                v.tensor_tensor_scan(xd_t[:, buf], same[:, buf], ps_inj[:], xd_t[:, 1 - buf, COLS - 1:COLS],
                                     ALU.mult, ALU.add).then_inc(s_scan, 1)

            def layer_norm(t, rnd, h, buf):
                m = small[:, buf]
                then(v.tensor_reduce(m[:, 0], by_node(t), AX.X, ALU.add))
                then(v.tensor_scalar(m[:, 1], m[:, 0], -1.0 / D, None, ALU.mult))
                then(v.tensor_tensor(t, by_node(t), along(m[:, 1], D), ALU.add))
                then(v.tensor_tensor(tmp[:], t, t, ALU.mult))
                then(v.tensor_reduce(m[:, 3], by_node(tmp[:]), AX.X, ALU.add))
                v.tensor_scalar(m[:, 2], m[:, 3], 1.0 / D, EPS, ALU.mult, ALU.add).then_inc(s_lnv, 1)
                dve.wait_ge(s_lnr, cdone(rnd, h, buf))
                then(v.reciprocal(m[:, 4], m[:, 2]))
                return v.tensor_tensor(t, by_node(t), along(m[:, 4], D), ALU.mult)

            for layer in range(2):
                def carry(h, buf):
                    carry_dst(layer, h, buf)

                def fold(h, buf):
                    dve.wait_ge(s_gates, done(layer, h, buf))
                    v.tensor_scalar(gv[:, buf, 0], ps_gv[:, buf, 0], GATE_MIN, None, ALU.max).then_inc(s_fold, 1)

                def messages(h, buf):
                    dve.wait_ge(s_lns, done(layer, h, buf))
                    v.scalar_tensor_tensor(soft, ps_gv[:, buf, 1], 0.0, gv[:, buf, 1], ALU.max,
                                           ALU.add).then_inc(s_soft, 1)
                    dve.wait_ge(s_soft, done(layer, h, buf))
                    v.tensor_tensor(msg, gv[:, buf, 0], soft, ALU.mult).then_inc(s_msg, 1)
                    dve.wait_ge(s_msg, done(layer, h, buf))
                    dve.wait_ge(s_turned, done(layer, h, buf, 2))
                    dve.wait_ge(s_sumt, done(layer, h, buf, 1))
                    dve.wait_ge(s_same_sum[buf], loaded_one(32, layer, h))
                    v.tensor_tensor_scan(sum_t[:, buf], same_sum[:, buf], msg, sum_t[:, 1 - buf, COLS - 1:COLS],
                                         ALU.mult, ALU.add).then_inc(s_sumt, 1)

                pipeline(dve, (carry, 0), (messages, 2), (fold, 1))

                def stage_get(h, buf):
                    v.tensor_scalar(get_nodes[:, buf], last_idx[:, ccols(h, buf)], 0.0, None,
                                    ALU.add).then_inc(s_gnodes, 1)

                def add_sums(h, buf):
                    hc = H[:, chunk(h, buf)]
                    then(v.tensor_tensor(by_node(tmp[:]), along(seam[:, ccols(h, buf)], D),
                                         across(seam_row[:], CH), ALU.mult))
                    dve.wait_ge(s_agg[buf], h * (16 * CH) + 16 * CH * (layer * CP + 1))
                    then(v.tensor_tensor(hc, hc, agg[:, buf], ALU.add))
                    then(v.tensor_tensor(hc, hc, tmp[:], ALU.add))
                    then(v.tensor_tensor(total[:], total[:], hc, ALU.add))

                dve.wait_ge(s_seam, 16 * (layer + 1))
                if layer:
                    dve.wait_ge(s_pads, 16)
                steps.begin()
                then(v.memset(total[:], 0.0))
                stage_get(0, 0)
                stage_get(0, 1)
                steps.end()
                with dve.Fori(0, CP - 1) as i:
                    steps.begin(i, 8)
                    for buf in range(2):
                        add_sums(i, buf)
                        stage_get(i + 1, buf)
                steps.end(CP - 1, 8)
                steps.begin()
                for buf in range(2):
                    add_sums(CP - 1, buf)
                dve.sem_inc(s_part, 1)
                dve.wait_ge(s_tot, 2 * layer + 1)
                then(v.tensor_reduce(stat[:, 0], ps_out[:, 0:CW].rearrange("p (c f) -> p f c", f=D), AX.X, ALU.add))
                then(v.scalar_tensor_tensor(stat[:, 1], stat[:, 0], -1.0 / N, norm_w[:, layer, 2], ALU.mult, ALU.mult))
                then(v.tensor_tensor(by_node(H[:]), by_node(H[:]), across(stat[:, 1], NT), ALU.add))
                then(v.tensor_tensor(squares, H[:], H[:], ALU.mult))
                v.tensor_reduce(stat[:, 2], squares.rearrange("p (t f) -> p f t", f=D), AX.X,
                                ALU.add).then_inc(s_part, 1)
                dve.wait_ge(s_tot, 2 * layer + 2)
                then(v.tensor_tensor(stat[:, 3], stat[:, 1], stat[:, 1], ALU.mult))
                then(v.scalar_tensor_tensor(stat[:, 3], stat[:, 3], float(N - NP), ps_out[:, 0:D], ALU.mult, ALU.add))
                v.tensor_scalar(stat[:, 4], stat[:, 3], 1.0 / N, EPS, ALU.mult, ALU.add).then_inc(s_var, 1)
                dve.wait_ge(s_std, layer + 1)
                then(v.reciprocal(stat[:, 5], stat[:, 4]))
                then(v.tensor_tensor(stat[:, 6], stat[:, 5], norm_w[:, layer, 0], ALU.mult))
                steps.end()

                with dve.Fori(0, CP) as i:
                    steps.begin(i, 4 if layer == 0 else 20)
                    for buf in range(2):
                        hc = H[:, chunk(i, buf)]
                        stage_idx(layer + 1, i, buf)
                        then(v.tensor_tensor(by_node(tmp[:]), by_node(hc), across(stat[:, 6], CH), ALU.mult))
                        then(v.tensor_tensor(by_node(tmp[:]), by_node(tmp[:]), across(norm_w[:, layer, 1], CH), ALU.add))
                        if layer == 0:
                            dve.wait_ge(s_table[buf], tabled(0, i, 1))
                            dve.wait_ge(s_hcopy, cdone(0, i, buf, 2))
                            v.scalar_tensor_tensor(stage[:, buf], tmp[:], SLOPE, tmp[:], ALU.mult,
                                                   ALU.max).then_inc(s_stage, 1)
                            dve.wait_ge(s_stage, cdone(1, i, buf))
                            continue
                        dve.wait_ge(s_zt, cdone(0, i, buf, 2))
                        dve.wait_ge(s_hcopy, cdone(1, i, buf, 2))
                        then(v.scalar_tensor_tensor(z[:, buf], tmp[:], SLOPE, tmp[:], ALU.mult, ALU.max))
                        then(v.tensor_tensor(z[:, buf], z[:, buf], X[:, chunk(i, buf)], ALU.add))
                        layer_norm(z[:, buf], 0, i, buf).then_inc(s_z, 1)
                steps.end(CP, 4 if layer == 0 else 20)

            drop_node, src_all = drop[:, 1:2], src_f
            def last_layer(i):
                for buf in range(2):
                    carry_dst(2, i, buf)
                    dve.wait_ge(s_idx[buf], i * 16 + 16 * (2 * PAIRS + 1))
                    dve.wait_ge(s_srcb, done(0, i, buf, 2))
                    v.tensor_copy(src_f[:, buf], idx[:, buf]).then_inc(s_srcf, 1)
                    dve.wait_ge(s_srcf, done(0, i, buf))
                    dve.wait_ge(s_srcb, done(0, i, buf))
                    dve.wait_ge(s_comb, done(0, i, buf, 2))
                    equal_now = equal[:, buf].rearrange("p (k e) -> p k e", e=P)
                    v.tensor_tensor(equal_now, ps_gv[:, buf].rearrange("p k (t e) -> p (k t) e", e=P),
                                    along(src_f[:, buf], P), ALU.is_equal).then_inc(s_equal, 1)
                    dve.wait_ge(s_equal, done(0, i, buf))
                    then(v.tensor_tensor(earlier, equal_now, across(before[:], SLOTS), ALU.mult))
                    then(v.tensor_reduce(dots[:, 6], earlier, AX.X, ALU.add))
                    then(v.tensor_scalar(dots[:, 7], src_f[:, buf], drop_node, None, ALU.subtract))
                    then(v.scalar_tensor_tensor(dots[:, 8], dots[:, 6], 0.0, dots[:, 7], ALU.is_equal, ALU.mult))
                    put_before(dve, i, buf)
                    v.tensor_scalar(put_idx[:, buf], dots[:, 8], drop_node, None, ALU.add).then_inc(s_pidx, 1)
                    dve.wait_ge(s_wc, done(0, i, buf))
                    dve.wait_ge(s_gath[buf], gathered(2, i))
                    then(v.tensor_tensor(prod, G[:, buf], wc[:, buf], ALU.mult))
                    then(v.tensor_reduce(dots[:, 0], by_node(prod), AX.X, ALU.add))
                    dve.wait_ge(s_sq, done(0, i, buf))
                    v.tensor_reduce(dots[:, 1:3].rearrange("p a k -> p (a k)"), by_node(sq), AX.X, ALU.add).then_inc(s_used, 1)
                    dve.wait_ge(s_used, done(0, i, buf))
                    then(v.tensor_tensor(dots[:, 4], dots[:, 1], dots[:, 2], ALU.mult))
                    v.tensor_scalar(dots[:, 3], dots[:, 4], SIM_EPS * SIM_EPS, None, ALU.max).then_inc(s_n2, 1)
                    dve.wait_ge(s_nn, done(0, i, buf))
                    then(v.reciprocal(dots[:, 5], dots[:, 3]))
                    then(v.tensor_tensor(dots[:, 9], dots[:, 0], dots[:, 5], ALU.mult))
                    then(v.tensor_scalar(dots[:, 10], dots[:, 9], 0.0, coef[:, 8:9], ALU.max, ALU.mult))
                    then(v.tensor_scalar(dots[:, 11], dots[:, 9], 0.0, coef[:, 9:10], ALU.min, ALU.mult))
                    then(v.tensor_tensor(dots[:, 10], dots[:, 10], dots[:, 11], ALU.add))
                    then(v.tensor_tensor(dots[:, 9], dots[:, 10], weight[:, ds(i * (2 * SLOTS) + buf * SLOTS, SLOTS)],
                                         ALU.mult))
                    v.tensor_tensor(w_msg[:, buf], by_node(wc[:, buf]), along(dots[:, 9], D), ALU.mult).then_inc(s_wm, 1)

            steps.begin()
            last_layer(0)
            steps.end()
            with dve.Fori(1, PAIRS) as i:
                steps.begin(i - 1, 26)
                last_layer(i)
            steps.end(PAIRS - 1, 26)

            with dve.Fori(0, CP) as i:
                steps.begin(i, 20)
                for buf in range(2):
                    part = [fin[:, buf, a] for a in range(ACCS)]
                    t = z[:, buf]
                    dve.wait_ge(s_fin[buf], i * (16 * ACCS) + 16 * ACCS)
                    dve.wait_ge(s_out_st[buf], i * 16 + 16)
                    then(v.tensor_tensor(t, part[0], part[1], ALU.add))
                    then(v.tensor_tensor(t, t, part[2], ALU.add))
                    v.tensor_tensor(t, t, part[3], ALU.add).then_inc(s_fused, 1)
                    dve.wait_ge(s_fused, cdone(0, i, buf))
                    then(v.scalar_tensor_tensor(t, X[:, chunk(i, buf)], coef[:, 10:11], t, ALU.mult, ALU.add))
                    then(v.tensor_tensor(t, t, H[:, chunk(i, buf)], ALU.add))
                    layer_norm(t, 1, i, buf).then_inc(s_result, 1)
                steps.end(CP, 20)


_OUT = (N, D)


def kernel(**inputs):
    import concourse.bacc as bacc
    from concourse.bass_utils import run_bass_kernel_spmd

    a = {k: np.asarray(w) for k, w in inputs.items()}

    def edges(w, fill):
        padded = np.full((EP,) + w.shape[1:], fill, w.dtype)
        padded[:E] = w
        return padded

    def by_slot(w):
        return np.ascontiguousarray(w.reshape(2, GROUPS, P, TILES).transpose(2, 1, 3, 0).reshape(P, -1))

    x = np.zeros((NP, D), a["x"].dtype)
    x[:N] = a["x"]
    src, dst = edges(a["src"], 0), edges(a["dst"], N)
    dst_prev = np.concatenate([np.full(1, -1, dst.dtype), dst[:-1]])
    dst_prev[HALF] = -1
    attr = edges(a["edge_attr_32"], 0).reshape(2, GROUPS, COLS, DA).transpose(1, 0, 3, 2)
    arrays = {
        "x": x, "dst_rows": dst.reshape(P, EP // P), "dst_blocks": dst.reshape(SEARCH, SEARCH),
        "dst_prev": dst_prev.reshape(P, EP // P), "block_last": dst.reshape(SEARCH, SEARCH)[:, -1].reshape(1, SEARCH),
        "seam_dst": dst[HALF:HALF + 1].reshape(1, 1), "src_g": by_slot(src), "dst_e": by_slot(dst),
        "adj_e": by_slot(edges(a["edge_weight"], 0)), "deg_e": by_slot(edges(a["edge_weight_n2"], 0)),
        "attr_t": attr.reshape(GROUPS, 2 * DA, COLS),
    }
    for layer in (1, 2):
        for name in ("Wf", "bf", "Ws", "bs", "gw", "gb", "gm"):
            w = a[f"L0_gnn_{name}{layer}"]
            arrays[f"{name}{layer}"] = w if w.ndim == 2 else w.reshape(1, -1)
    arrays["W"] = a["L1_gnn_W"]
    for name in ("b", "deg_coeff", "coeff_param", "scale_param"):
        arrays[name] = a[f"L1_gnn_{name}"].reshape(1, -1)
    arrays = {k: np.ascontiguousarray(w) for k, w in arrays.items()}

    nc = bacc.Bacc("TRN2", target_bir_lowering=False, num_devices=1)
    ap = {k: nc.dram_tensor(f"in_{k}", w.shape, mybir.dt.from_np(w.dtype), kind="ExternalInput").ap()
          for k, w in arrays.items()}
    out = nc.dram_tensor("out", [NP, D], F32, kind="ExternalOutput").ap()
    conv = [[ap[f"{name}{layer}"] for name in ("Wf", "bf", "Ws", "bs", "gw", "gb", "gm")] for layer in (1, 2)]
    gnn(nc, ap["x"], ap["dst_rows"], ap["dst_blocks"], ap["dst_prev"], ap["block_last"], ap["seam_dst"],
        ap["src_g"], ap["src_g"], ap["dst_e"], ap["adj_e"], ap["deg_e"], ap["attr_t"], conv, ap["W"], ap["b"],
        ap["deg_coeff"], ap["coeff_param"], ap["scale_param"], out)
    result = run_bass_kernel_spmd(nc, [{f"in_{k}": w for k, w in arrays.items()}], core_ids=[0])
    return result.results[0]["out"][:N]
```

```python
from contextlib import ExitStack

import numpy as np

import concourse.bass as bass
from concourse import mybir

P = 128
N, E, D, DA = 12500, 200000, 64, 32
TILES = 4
COLS = TILES * P
NT = -(-N // P)
NP = NT * P
GROUPS = 2 * (-(-E // (4 * COLS)))
PAIRS = GROUPS // 2
HALF = GROUPS * COLS
EP = 2 * HALF
SLOTS = 2 * TILES
CH = 7
CHUNKS = NT // CH
CP = CHUNKS // 2
CW = CH * D
SEARCH = 448
ACCS = 4
AHEAD = 1
RUNS = SLOTS // ACCS
AROWS = NP + P
PADS_FROM = (N - (P - 1) * NT) * D
ZW = AROWS // P * D // 2
ZI = 28 * D
CLEARS = EP // P * D // ZI
GATE_MIN = -44.0
EPS = 1e-5
SIM_EPS = 1e-8
SLOPE = 0.01

assert NT % (2 * CH) == 0 and SEARCH * SEARCH == EP and RUNS == 2 and N > (P - 1) * NT

ALU = mybir.AluOpType
ACT = mybir.ActivationFunctionType
AX = mybir.AxisListType
F32 = mybir.dt.float32
I32 = mybir.dt.int32
BF16 = mybir.dt.bfloat16
ds = bass.ds


class Steps:

    def __init__(self, engine, sem):
        self.engine, self.sem, self.total, self.k, self.at = engine, sem, 0, 0, 0

    def begin(self, trip=0, per=0):
        self.at, self.k = self.total + trip * per, 0

    def end(self, trips=1, per=None):
        assert per is None or per == self.k, (per, self.k)
        self.total += trips * self.k
        self.at, self.k = self.total, 0

    def then(self, instruction):
        self.k += 1
        instruction.then_inc(self.sem, 1)
        self.engine.wait_ge(self.sem, self.at + self.k)


def gnn(nc, x, dst_rows, dst_blocks, dst_prev, block_last, seam_dst, src_g, src_e, src_ahead, dst_e, adj_e, deg_e,
        attr_t, conv, W, b, deg_coeff, coeff_param, scale_param, out):
    with ExitStack() as ctx:
        def sb(name, shape, dt=F32):
            return ctx.enter_context(nc.sbuf_tensor(name, shape, dt))

        def psum(name, shape):
            return ctx.enter_context(nc.psum_tensor(name, shape, F32))

        def sem(name):
            return ctx.enter_context(nc.semaphore(name))

        def two(name):
            return [sem(f"{name}_{i}") for i in range(2)]

        def dram(name, shape, dt=F32):
            return nc.dram_tensor(name, shape, dt).ap()

        inj_d = dram("first_edge_rows", [EP + P, D])
        sums_d = dram("running_sums", [EP + 1, D])
        ahead_d = dram("rows_gathered_ahead", [PAIRS * P, D])
        same_d = dram("same_dst", [EP], BF16)
        h_d = dram("h_rows", [NP, D])
        wh_d = dram("wh_rows", [NP, D])
        acc_d = [dram(f"by_src_{a}", [AROWS, D]) for a in range(ACCS)]
        inj_groups = inj_d[0:EP].rearrange("(g p r) f -> g p (r f)", p=P, r=SLOTS)
        sums_groups = sums_d[0:EP].rearrange("(g p r) f -> g p (r f)", p=P, r=SLOTS)
        ahead_pairs = ahead_d.rearrange("(n p) f -> p n f", p=P)
        same_groups = same_d.rearrange("(g c) -> g c", c=COLS)

        ident = sb("ident", [P, P])
        ones = sb("ones", [P, P])
        before = sb("before", [P, P])
        zeros = sb("zeros", [P, ZW])
        node_id_i = sb("node_id_i", [P, NT + 1], I32)
        node_id = sb("node_id", [P, NT + 1])
        drop_i = sb("drop_i", [P, 2], I32)
        drop = sb("drop", [P, 2])
        w_dst = sb("w_dst", [P, 2, 2, P])
        w_src = sb("w_src", [P, 2, 2, P])
        w_attr = sb("w_attr", [2 * DA + 1, 2, 2, P])
        norm_w = sb("norm_w", [P, 2, 3, D])
        w_lin = sb("w_lin", [D + 1, D])
        coef_in = sb("coef_in", [P, 6])
        coef = sb("coef", [P, 16])
        last_idx = sb("last_idx", [P, NT])
        first_idx = sb("first_idx", [P, NT])
        seam = sb("seam", [P, NT])
        seam_idx = sb("seam_idx", [P, 1], I32)
        weight = sb("weight", [P, GROUPS * SLOTS])
        H = sb("H", [P, NT * D])
        X = sb("X", [P, NT * D])
        put_nodes = sb("put_nodes", [P, 2, CH], I32)
        get_nodes = sb("get_nodes", [P, 2, CH], I32)
        stage = sb("stage", [P, 2, CW])
        agg = sb("agg", [P, 2, CW])
        z = sb("z", [P, 2, CW])
        tmp = sb("tmp", [P, CW])
        total = sb("total", [P, CW])
        stat = sb("stat", [P, 8, D])
        small = sb("small", [P, 2, 5, CH])
        x2_t = sb("x2_t", [D + 1, 2, CH * P])
        seam_get = sb("seam_get", [P, D])
        seam_row = sb("seam_row", [P, D])
        idx = sb("idx", [P, 2, SLOTS], I32)
        inj = sb("inj", [P, 2, SLOTS * D])
        same = sb("same", [P, 2, COLS], BF16)
        same_sum = sb("same_sum", [P, 2, COLS], BF16)
        attr = sb("attr", [2 * DA + 1, 2, COLS])
        G = sb("G", [P, 2, SLOTS * D])
        xd_t = sb("xd_t", [P, 2, COLS])

        arena = sb("arena", [P, 17600])

        def carve():
            at = [0]

            def tile(*shape, dt=F32):
                n = int(np.prod(shape))
                view = arena[:, at[0]:at[0] + n]
                at[0] += n
                if dt != F32:
                    view = view.bitcast(dt)
                names = "abc"[:len(shape)]
                sizes = dict(zip(names[1:], shape[1:]))
                return view.rearrange(f"p ({' '.join(names)}) -> p {' '.join(names)}", **sizes) if len(shape) > 1 else view
            return tile

        tile = carve()
        dst_now, dst_was, src_i, dst_i = (tile(GROUPS * SLOTS, dt=I32) for _ in range(4))
        deg, deg_tmp = tile(GROUPS * SLOTS), tile(GROUPS * SLOTS)
        last_i, last_f, junk = tile(SEARCH, dt=I32), tile(SEARCH), tile(SEARCH)
        block_rows = tile(2, CH, SEARCH, dt=I32)
        search = tile(2, 3, CH)
        first, valid, row = tile(NT + 1), tile(NT), tile(NT)
        same_all = sb("same_all", [P, EP // P], BF16)
        block_idx = sb("block_idx", [P, 2, CH], I32)

        tile = carve()
        squares = tile(NT * D)
        xs_t = tile(2, COLS)
        gv = tile(2, 2, COLS)
        soft, msg = tile(COLS), tile(COLS)
        sum_t = tile(2, COLS)
        sums = tile(2, SLOTS * D)

        tile = carve()
        wc = tile(2, SLOTS * D)
        prod = tile(SLOTS * D)
        sq = tile(2 * SLOTS * D)
        dots = tile(12, SLOTS)
        src_f = tile(2, SLOTS)
        equal = tile(2, SLOTS * P)
        earlier = tile(SLOTS, P)
        w_msg = tile(2, SLOTS * D)
        put = tile(2, SLOTS * D)
        fin = tile(2, ACCS, CW)
        put_idx = sb("put_idx", [P, 2, SLOTS], I32)

        ps_inj = psum("ps_inj", [P, COLS])
        ps_g = psum("ps_g", [P, COLS])
        ps_gv = psum("ps_gv", [P, 2, 2, COLS])
        ps_out = psum("ps_out", [P, COLS])

        s_nodes = sem("x_loaded")
        s_search = sem("search_inputs_loaded")
        s_edges = sem("edge_scalars_loaded")
        s_weights = sem("weights_loaded")
        s_zeros = sem("zeros_set")
        s_tiles = sem("weight_tiles_zeroed")
        s_pool = sem("pool_constants")
        s_cleared = two("first_edge_rows_cleared")
        s_tables = sem("by_src_tables_cleared")
        s_zero_row = sem("zero_row_cleared")
        s_same_set = sem("same_set")
        s_same = sem("same_stored")
        s_dve = sem("dve_steps")
        s_act = sem("act_steps")
        s_ptick = sem("pool_waited")
        s_atick = sem("act_waited")
        s_petick = sem("pe_waited")
        s_bidx = sem("block_idx_ready")
        s_rows = two("block_rows_gathered")
        s_end_idx = sem("end_block_idx_ready")
        s_end_rows = sem("end_block_gathered")
        s_deg = sem("deg_ready")
        s_dega = sem("deg_activated")
        s_setup = sem("setup_done")
        s_pnodes = sem("put_nodes_ready")
        s_stage = sem("stage_ready")
        s_scat = sem("node_columns_scattered")
        s_table = two("chunk_stored")
        s_gnodes = sem("get_nodes_ready")
        s_agg = two("agg_gathered")
        s_part = sem("partition_sums")
        s_tot = sem("node_sums")
        s_var = sem("variance_ready")
        s_std = sem("std_ready")
        s_hcopy = sem("h_copied")
        s_seam = sem("seam_sums_loaded")
        s_sget = sem("seam_row_gathered")
        s_sput = sem("seam_row_put")
        s_pads = sem("padded_nodes_zeroed")
        s_lnv = sem("ln_variance_ready")
        s_lnr = sem("ln_root_ready")
        s_z = sem("x2_ready")
        s_zt = sem("x2_turned")
        s_ztc = sem("x2_turned_copied")
        s_wh = sem("wh_ready")
        s_base = sem("base_added")
        s_centred = sem("half_centred")
        s_squared = sem("half_squared")
        s_whc = sem("wh_copied")
        s_fin = two("by_src_loaded")
        s_fused = sem("by_src_used")
        s_result = sem("result_ready")
        s_out_st = two("result_stored")
        s_aidx = two("ahead_idx_loaded")
        s_ahead = two("gathered_ahead")
        s_ahead_st = two("ahead_stored")
        s_ahead_in = sem("ahead_loaded")
        s_idx = two("idx_loaded")
        s_load = two("group_loaded")
        s_attr = two("attr_loaded")
        s_same_sum = two("same_loaded_again")
        s_gath = two("src_rows_gathered")
        s_injt = sem("inj_turned")
        s_scan = sem("dst_rows_carried")
        s_gt = sem("src_rows_turned")
        s_xs = sem("src_rows_copied")
        s_gates = sem("gates_ready")
        s_fold = sem("gates_clamped")
        s_soft = sem("softplus_ready")
        s_lns = sem("gates_activated")
        s_msg = sem("messages_ready")
        s_sumt = sem("messages_summed")
        s_turned = sem("sums_turned")
        s_sums = sem("sums_copied")
        s_stored = two("sums_stored")
        s_wt = sem("wc_turned")
        s_wc = sem("wc_copied")
        s_sq = sem("squares_ready")
        s_n2 = sem("norm_products_ready")
        s_nn = sem("norm_product_roots")
        s_used = sem("src_rows_used")
        s_srcf = sem("src_float")
        s_srcb = sem("src_spread")
        s_equal = sem("equal_ready")
        s_pidx = sem("put_idx_ready")
        s_wm = sem("weighted_ready")
        s_comb = sem("combined")
        s_put = sem("put_ready")
        s_added = two("added")

        by_two = [s_bidx, s_pnodes, s_stage, s_gnodes, s_hcopy, s_lnv, s_lnr, s_z, s_zt, s_ztc, s_wh, s_whc,
                  s_fused, s_result, s_injt, s_scan, s_gt, s_xs, s_gates, s_fold, s_soft, s_lns, s_msg,
                  s_sumt, s_turned, s_sums, s_wt, s_wc, s_sq, s_n2, s_nn, s_used, s_srcf, s_srcb,
                  s_equal, s_pidx, s_wm, s_comb, s_put]
        by_sp = [s_ahead_st, s_table, s_out_st, s_stored]

        def done(rnd, h, buf, back=0):
            return h * 2 + (rnd * GROUPS + buf + 3 - back)

        def cdone(rnd, h, buf, back=0):
            return h * 2 + (rnd * CHUNKS + buf + 3 - back)

        def scattered(rnd, h, buf, column=CH):
            return h * (32 * CH) + 16 * (rnd * NT + buf * CH + column)

        def tabled(rnd, h, back=0):
            return h * 16 + 16 * (rnd * CP + 2 - back)

        def stored(rnd, h, back=0):
            return h * 16 + 16 * (rnd * PAIRS + 2 - back)

        def loaded(layer, h):
            return h * 48 + 48 * (layer * PAIRS + 1)

        def loaded_one(amount, layer, h):
            return h * amount + amount * (layer * PAIRS + 1)

        def gathered(layer, h, buf):
            def per(k):
                return 16 * (SLOTS - buf) if k < AHEAD else 16 * SLOTS
            return h * per(layer) + (sum(per(k) for k in range(layer)) * PAIRS + per(layer))

        def added(h, buf, run):
            return h * (16 * SLOTS) + 16 * (buf * SLOTS + run * ACCS) // 2

        def put_before(engine, h, buf):
            for half in range(2):
                if not at_start(h):
                    engine.wait_ge(s_added[half], added(h, buf, 0) - 8 * SLOTS)

        def at_start(h):
            return isinstance(h, int) and h == 0

        def all_trips(engine, body, trips):
            body(0)
            with engine.Fori(1, trips) as i:
                body(i)

        def chunk(h, buf):
            return ds(h * (2 * CW) + buf * CW, CW)

        def ccols(h, buf):
            return ds(h * (2 * CH) + buf * CH, CH)

        halves = [slice(k * (NT // 2) * D, (k + 1) * (NT // 2) * D) for k in range(2)]

        def nodes(ap):
            return ap.rearrange("(p t) f -> p (t f)", p=P)

        def by_node(ap):
            return ap.rearrange("p (c f) -> p c f", f=D)

        def across(ap, n):
            return ap.unsqueeze(1).to_broadcast([P, n, ap.shape[1]])

        def along(ap, n):
            return ap.unsqueeze(2).to_broadcast([P, ap.shape[1], n])

        def turned(ap, j):
            return ap.rearrange("p (q j) -> p q j", j=TILES)[:, :, j]

        def pipeline(engine, *stages, steps=None, per=0, pairs=PAIRS, peel=0):
            def step(i, buf):
                for stage_, lag in stages:
                    h = i + (buf - lag) // 2
                    if not isinstance(h, int) or 0 <= h < pairs:
                        stage_(h, (buf - lag) % 2)

            lags = [lag for _, lag in stages]
            head, tail = max(1, -(-max(lags) // 2)) + peel, pairs - -(min(lags) // 2)
            if steps:
                steps.begin()
            for k in range(2 * head):
                step(k // 2, k % 2)
            if steps:
                steps.end()
            with engine.Fori(head, tail) as i:
                if steps:
                    steps.begin(i - head, per)
                step(i, 0)
                step(i, 1)
            if steps:
                steps.end(tail - head, per)
                steps.begin()
            for k in range(2 * tail, 2 * pairs + max(lags)):
                step(k // 2, k % 2)
            if steps:
                steps.end()

        block = ctx.enter_context(nc.Block())

        @block.sync
        def _(sp):
            def load(out_, in_, s):
                sp.dma_start(out_, in_).then_inc(s, 16)

            load(last_i, block_last.to_broadcast([P, SEARCH]), s_search)
            load(dst_now, dst_rows, s_search)
            load(dst_was, dst_prev, s_search)
            load(X[:], nodes(x), s_nodes)
            load(H[:], nodes(x), s_nodes)
            load(dst_i, dst_e, s_edges)
            load(src_i, src_e, s_edges)
            load(weight[:], adj_e, s_edges)
            load(deg, deg_e, s_edges)
            load(seam_idx[:], seam_dst.to_broadcast([P, 1]), s_edges)
            load(coef_in[:, 0:2], deg_coeff.to_broadcast([P, 2]), s_edges)
            load(coef_in[:, 2:5], coeff_param.to_broadcast([P, 3]), s_edges)
            load(coef_in[:, 5:6], scale_param.to_broadcast([P, 1]), s_edges)
            def ahead_idx(h, buf):
                if not at_start(h):
                    sp.wait_ge(s_ahead[buf], h * (16 * CH))
                load(get_nodes[:, buf], src_ahead[:, ccols(h, buf)], s_aidx[buf])

            def ahead_store(h, buf):
                sp.wait_ge(s_ahead[buf], h * (16 * CH) + 16 * CH)
                load(ahead_pairs[:, ccols(h, buf)], by_node(agg[:, buf]), s_ahead_st[buf])

            pipeline(sp, (ahead_idx, 0), (ahead_store, 1), pairs=CP)
            for buf in range(2):
                sp.wait_ge(s_ahead_st[buf], 16 * (CP + 1))

            sp.wait_ge(s_same_set, 1)
            load(same_d.rearrange("(p c) -> p c", p=P), same_all[:], s_same)
            sp.wait_ge(s_tiles, 1)
            for layer, (Wf, bf, Ws, bs, gw, gb, gm) in enumerate(conv):
                for k, (w, bias) in enumerate(((Wf, bf), (Ws, bs))):
                    for s in range(2):
                        o = slice(s * D, (s + 1) * D)
                        load(w_dst[o, layer, k, o], w[0:D, :], s_weights)
                        load(w_src[o, layer, k, o], w[D:2 * D, :], s_weights)
                        load(w_attr[s * DA:(s + 1) * DA, layer, k, o], w[2 * D:, :], s_weights)
                        load(w_attr[2 * DA:2 * DA + 1, layer, k, o], bias, s_weights)
                for k, v in enumerate((gw, gb, gm)):
                    load(norm_w[:, layer, k, :], v.to_broadcast([P, D]), s_weights)
            load(w_lin[0:D, :], W, s_weights)
            load(w_lin[D:D + 1, :], b, s_weights)
            sp.wait_ge(s_same, 16)

            for layer in range(3):
                sp.wait_ge(s_scat, 16 * NT * (layer + 1))
                sp.wait_ge(s_sget, 16 * (layer + 1))
                load(inj_d[1:2, :], seam_get[0:1, :], s_sput)
                sp.wait_ge(s_sput, 16 * (layer + 1))

                def load_idx(h, buf):
                    if not at_start(h):
                        if layer < 2:
                            sp.wait_ge(s_gath[buf], gathered(layer, h - 1, buf))
                        else:
                            sp.wait_ge(s_used, done(0, h, buf, 2))
                    load(idx[:, buf], src_g[:, ds((h * 2 + buf) * SLOTS, SLOTS)], s_idx[buf])

                def load_rows(h, buf):
                    g = h * 2 + buf
                    sp.wait_ge(s_scan, done(layer, h, buf, 2))
                    load(inj[:, buf], inj_groups[ds(g, 1)].rearrange("a p c -> p (a c)"), s_load[buf])
                    load_same(same, s_load, g, buf)

                def load_ahead(h, buf):
                    if buf and layer < AHEAD:
                        sp.wait_ge(s_gt, done(layer, h, buf, 2))
                        load(G[:, buf, (SLOTS - 1) * D:], ahead_pairs[:, ds(h, 1)].rearrange("p a f -> p (a f)"),
                             s_ahead_in)

                def load_attr(h, buf):
                    sp.wait_ge(s_gates, done(layer, h, buf, 2))
                    load(attr[0:2 * DA, buf], attr_t[ds(h * 2 + buf, 1)].rearrange("a k c -> k (a c)"), s_attr[buf])

                def load_same(tile_, s, g, buf):
                    for half in range(2):
                        load(tile_[half * D:(half + 1) * D, buf],
                             same_groups[ds(g + half * GROUPS, 1), :].to_broadcast([D, COLS]), s[buf])

                def load_again(h, buf):
                    sp.wait_ge(s_sumt, done(layer, h, buf, 2))
                    load_same(same_sum, s_same_sum, h * 2 + buf, buf)

                def store_sums(h, buf):
                    g = h * 2 + buf
                    sp.wait_ge(s_sums, done(layer, h, buf))
                    load(sums_groups[ds(g, 1)].rearrange("a p c -> p (a c)"), sums[:, buf], s_stored[buf])

                load_idx(0, 0)
                load_rows(0, 0)
                if layer == 2:
                    load_idx(0, 1)
                    pipeline(sp, (load_rows, -1), (load_idx, -2))
                    break
                pipeline(sp, (load_idx, -1), (load_rows, -1), (load_ahead, 0), (load_attr, 1), (load_again, 2),
                         (store_sums, 4))
                for buf in range(2):
                    sp.wait_ge(s_stored[buf], stored(layer, PAIRS - 1))
                load(seam_row[:], sums_d[EP - 2:EP - 1, :].to_broadcast([P, D]), s_seam)
                table_out = nodes((h_d, wh_d)[layer])
                with sp.Fori(0, CP) as i:
                    for buf in range(2):
                        sp.wait_ge(s_stage, cdone(layer + 1, i, buf))
                        load(table_out[:, chunk(i, buf)], stage[:, buf], s_table[buf])
                if layer == 0:
                    sp.wait_ge(s_hcopy, cdone(0, CP - 1, 1))
                    load(H[P - 1:P, PADS_FROM:NT * D], zeros[0:1, 0:NT * D - PADS_FROM], s_pads)

            for half in range(2):
                sp.wait_ge(s_added[half], 8 * GROUPS * SLOTS)

            def load_sums(h, buf):
                sp.wait_ge(s_fused, cdone(0, h, buf, 2))
                for a in range(ACCS):
                    load(fin[:, buf, a], nodes(acc_d[a][0:NP])[:, chunk(h, buf)], s_fin[buf])

            def store_result(h, buf):
                sp.wait_ge(s_result, cdone(0, h, buf))
                load(nodes(out)[:, chunk(h, buf)], z[:, buf], s_out_st[buf])

            pipeline(sp, (load_sums, 0), (store_result, 2), pairs=CP)
            for buf in range(2):
                sp.wait_ge(s_out_st[buf], 16 * (CP + 1))

        @block.gpsimd
        def _(pool):
            pool.memset(ident[:], 0.0).then_inc(s_pool, 1)
            pool.memset(before[:], 1.0).then_inc(s_pool, 1)
            pool.wait_ge(s_pool, 2)
            pool.affine_select(out=ident[:], in_=ident[:], compare_op=ALU.not_equal, fill=1.0, base=0,
                               pattern=[[-1, P]], channel_multiplier=1).then_inc(s_pool, 1)
            pool.affine_select(out=before[:], in_=before[:], compare_op=ALU.is_gt, fill=0.0, base=0,
                               pattern=[[-1, P]], channel_multiplier=1).then_inc(s_pool, 1)
            pool.iota(node_id_i[:], pattern=[[1, NT + 1]], base=0, channel_multiplier=NT).then_inc(s_pool, 1)
            pool.iota(drop_i[:, 0:1], pattern=[[1, 1]], base=EP, channel_multiplier=1).then_inc(s_pool, 1)
            pool.iota(drop_i[:, 1:2], pattern=[[1, 1]], base=NP, channel_multiplier=1).then_inc(s_pool, 1)

            def wait(s, value):
                pool.wait_ge(s, value)
                pool.sem_inc(s_ptick, 1)

            def gather(out_, table_in, index, s):
                pool.indirect_dma_start(out_, None, table_in, bass.IndirectOffsetOnAxis(ap=index, axis=0)).then_inc(s, 16)

            def gather_ahead(begin, end):
                with pool.Fori(begin, end) as i:
                    for buf in range(2):
                        wait(s_aidx[buf], i * 16 + 16)
                        wait(s_ahead_st[buf], i * 16 + 16)
                        for c in range(CH):
                            gather(agg[:, buf, c * D:(c + 1) * D], x, get_nodes[:, buf, c:c + 1], s_ahead[buf])

            pool.wait_ge(s_end_idx, 1)
            gather(block_rows[:, 1, 0], dst_blocks, block_idx[:, 1, 0:1], s_end_rows)
            gather_ahead(0, CP // 2)

            def find_column(h, buf, c):
                if c == 0:
                    wait(s_bidx, cdone(0, h, buf))
                gather(block_rows[:, buf, c], dst_blocks, block_idx[:, buf, c:c + 1], s_rows[buf])

            def put_column(layer, h, buf, c):
                if c == 0:
                    wait(s_pnodes, cdone(layer, h, buf))
                    wait(s_stage, cdone(layer, h, buf))
                if layer or buf or c or not at_start(h):
                    wait(s_scat, scattered(layer, h, buf, c))
                else:
                    gather_ahead(CP // 2, CP)
                    for half in range(2):
                        pool.wait_ge(s_cleared[half], 8 * CLEARS)
                pool.indirect_dma_start(
                    inj_d, bass.IndirectOffsetOnAxis(ap=put_nodes[:, buf, c:c + 1], axis=0),
                    stage[:, buf, c * D:(c + 1) * D], None).then_inc(s_scat, 16)

            for layer in range(3):
                stages = []
                for c in range(CH):
                    if layer == 0:
                        stages.append((lambda h, buf, c=c: find_column(h, buf, c), 0))
                    stages.append((lambda h, buf, c=c: put_column(layer, h, buf, c), 0 if layer else 3))
                pipeline(pool, *stages, pairs=CP)
                table_in = (x, h_d, wh_d)[layer]
                if layer:
                    for buf in range(2):
                        pool.wait_ge(s_table[buf], tabled(layer - 1, CP - 1))
                else:
                    pool.wait_ge(s_edges, 16 * 8)
                if layer:
                    pool.wait_ge(s_sput, 16 * layer)
                gather(seam_get[:], table_in, seam_idx[:], s_sget)

                def gather_group(h, buf, first=0, to=SLOTS):
                    if first == 0:
                        wait(s_idx[buf], h * 16 + 16 * (layer * PAIRS + 1))
                        if layer < 2:
                            wait(s_gt, done(layer, h, buf, 2))
                        else:
                            wait(s_used, done(0, h, buf, 2))
                    for k in range(first, to):
                        if layer < AHEAD and buf and k == SLOTS - 1:
                            continue
                        gather(G[:, buf, k * D:(k + 1) * D], table_in, idx[:, buf, k:k + 1], s_gath[buf])

                def add_run(h, buf, run):
                    if run == 0:
                        wait(s_pidx, done(0, h, buf))
                        wait(s_put, done(0, h, buf))
                    for a in range(ACCS):
                        half = a // (ACCS // 2)
                        if a % (ACCS // 2) == 0 and (run or buf or not at_start(h)):
                            wait(s_added[half], added(h, buf, run))
                        k = run * ACCS + a
                        pool.indirect_dma_start(
                            acc_d[a], bass.IndirectOffsetOnAxis(ap=put_idx[:, buf, k:k + 1], axis=0),
                            put[:, buf, k * D:(k + 1) * D], None, compute_op=ALU.add).then_inc(s_added[half], 16)

                if layer == 2:
                    pool.wait_ge(s_tables, 16 * 2 * ACCS)
                    split = SLOTS - ACCS // 2
                    pipeline(pool, (lambda h, buf: gather_group(h, buf, 0, split), 0),
                             (lambda h, buf: add_run(h, buf, 0), 2),
                             (lambda h, buf: gather_group(h, buf, split, SLOTS), 0),
                             (lambda h, buf: add_run(h, buf, 1), 2))
                    break
                with pool.Fori(0, PAIRS) as i:
                    for buf in range(2):
                        gather_group(i, buf)
                pool.wait_ge(s_zero_row, 16)
                for buf in range(2):
                    pool.wait_ge(s_stored[buf], stored(layer, PAIRS - 1))
                with pool.Fori(0, CP) as i:
                    for buf in range(2):
                        wait(s_gnodes, cdone(layer, i, buf))
                        for c in range(CH):
                            gather(agg[:, buf, c * D:(c + 1) * D], sums_d, get_nodes[:, buf, c:c + 1], s_agg[buf])

        @block.tensor
        def _(pe):
            pe.wait_ge(s_pool, 7)
            pe.wait_ge(s_weights, 16 * (2 * 19 + 2))

            def turn_inj(layer, h, buf):
                pe.wait_ge(s_load[buf], loaded(layer, h))
                pe.wait_ge(s_scan, done(layer, h, buf, 1))
                for j in range(TILES):
                    mm = pe.transpose(turned(ps_inj, j), inj[:, buf, j * P:(j + 1) * P], ident[:])
                mm.then_inc(s_injt, 1)

            for layer in range(2):
                def turn_rows(h, buf):
                    turn_inj(layer, h, buf)
                    pe.wait_ge(s_gath[buf], gathered(layer, h, buf))
                    if buf and layer < AHEAD:
                        pe.wait_ge(s_ahead_in, loaded_one(16, layer, h))
                    pe.wait_ge(s_xs, done(layer, h, buf, 1))
                    for j in range(TILES):
                        mm = pe.transpose(turned(ps_g, j), G[:, buf, j * P:(j + 1) * P], ident[:])
                    mm.then_inc(s_gt, 1)

                def products(h, buf):
                    pe.wait_ge(s_soft, done(layer, h, buf, 2))
                    pe.wait_ge(s_attr[buf], loaded_one(16, layer, h))
                    for k in range(2):
                        pe.matmul(ps_gv[:, buf, k], w_attr[:, layer, k], attr[:, buf], start=True, stop=False)
                    pe.wait_ge(s_xs, done(layer, h, buf))
                    for k in range(2):
                        pe.matmul(ps_gv[:, buf, k], w_src[:, layer, k], xs_t[:, buf], start=False, stop=False)
                    pe.wait_ge(s_scan, done(layer, h, buf))
                    for k in range(2):
                        mm = pe.matmul(ps_gv[:, buf, k], w_dst[:, layer, k], xd_t[:, buf], start=False, stop=True)
                    mm.then_inc(s_gates, 1)

                def turn_sums(h, buf):
                    pe.wait_ge(s_sumt, done(layer, h, buf))
                    pe.wait_ge(s_sums, done(layer, h, buf, 1))
                    for j in range(TILES):
                        mm = pe.transpose(ps_out[:, j * P:(j + 1) * P], turned(sum_t[:, buf], j), ident[:])
                    mm.then_inc(s_turned, 1)

                pipeline(pe, (turn_rows, 0), (products, 1), (turn_sums, 2))
                pe.wait_ge(s_part, 2 * layer + 1)
                pe.matmul(ps_out[:, 0:CW], ones[:], total[:], start=True, stop=True).then_inc(s_tot, 1)
                pe.wait_ge(s_part, 2 * layer + 2)
                pe.matmul(ps_out[:, 0:D], ones[:], stat[:, 2], start=True, stop=True).then_inc(s_tot, 1)

            with pe.Fori(0, CP) as i:
                for buf in range(2):
                    pe.wait_ge(s_z, cdone(0, i, buf))
                    pe.wait_ge(s_ztc, cdone(0, i, buf, 1))
                    pe.sem_inc(s_petick, 1)
                    for c in range(CH):
                        mm = pe.transpose(ps_gv[0:D, 0, c // TILES, c % TILES * P:(c % TILES + 1) * P],
                                          z[:, buf, c * D:(c + 1) * D], ident[:])
                    mm.then_inc(s_zt, 1)
                    pe.wait_ge(s_ztc, cdone(0, i, buf))
                    pe.wait_ge(s_whc, cdone(0, i, buf, 1))
                    for c in range(CH):
                        mm = pe.matmul(ps_out[:, c * D:(c + 1) * D], x2_t[:, buf, c * P:(c + 1) * P], w_lin[:],
                                       start=True, stop=True)
                    mm.then_inc(s_wh, 1)

            spread = ps_gv.rearrange("p b k (t e) -> p b (k t) e", e=P)

            def turn_src_dst(h, buf):
                turn_inj(2, h, buf)
                pe.wait_ge(s_srcf, done(0, h, buf))
                pe.wait_ge(s_equal, done(0, h, buf, 2))
                for k in range(SLOTS):
                    mm = pe.transpose(spread[:, buf, k], src_f[:, buf, k:k + 1].to_broadcast([P, P]), ident[:])
                mm.then_inc(s_srcb, 1)
                pe.wait_ge(s_scan, done(2, h, buf))
                pe.wait_ge(s_sq, done(0, h, buf, 1))
                for j in range(TILES):
                    mm = pe.transpose(ps_g[:, j * P:(j + 1) * P], turned(xd_t[:, buf], j), ident[:])
                mm.then_inc(s_wt, 1)

            def combine(h, buf):
                pe.wait_ge(s_equal, done(0, h, buf))
                pe.wait_ge(s_wm, done(0, h, buf))
                pe.wait_ge(s_put, done(0, h, buf, 1))
                for k in range(SLOTS):
                    mm = pe.matmul(ps_out[:, k * D:(k + 1) * D], equal[:, buf, k * P:(k + 1) * P],
                                   w_msg[:, buf, k * D:(k + 1) * D], start=True, stop=True)
                mm.then_inc(s_comb, 1)

            pipeline(pe, (turn_src_dst, 0), (combine, 1))

        @block.scalar
        def _(act):
            steps = Steps(act, s_act)
            act.wait_ge(s_zeros, 1)
            inj_rows = inj_d[0:EP].rearrange("(p r) f -> p (r f)", p=P)

            def clear_rows(i):
                for buf in range(2):
                    if not at_start(i):
                        act.wait_ge(s_cleared[buf], i * 16)
                    act.dma_start(inj_rows[:, ds(i * (2 * ZI) + buf * ZI, ZI)],
                                  zeros[:, 0:ZI]).then_inc(s_cleared[buf], 16)

            all_trips(act, clear_rows, CLEARS // 2)
            for buf in range(2):
                act.wait_ge(s_cleared[buf], 8 * CLEARS)
            act.dma_start(sums_d[EP:EP + 1, :], zeros[0:1, 0:D]).then_inc(s_zero_row, 16)

            def wait(s, value):
                act.wait_ge(s, value)
                act.sem_inc(s_atick, 1)

            act.wait_ge(s_deg, 1)
            steps.begin()
            steps.then(nc.scalar.activation(deg_tmp, deg_tmp, ACT.Exp))
            steps.then(nc.scalar.activation(coef[:, 0:4], coef[:, 0:4], ACT.Exp))
            steps.then(nc.scalar.activation(coef[:, 3:4], coef[:, 3:4], ACT.Ln, bias=1.0))
            nc.scalar.activation(deg_tmp, deg_tmp, ACT.Ln, bias=1.0).then_inc(s_dega, 1)
            steps.end()

            act.wait_ge(s_setup, 1)
            for layer in range(2):
                def copy_rows(h, buf):
                    act.wait_ge(s_gt, done(layer, h, buf))
                    act.wait_ge(s_gates, done(layer, h, buf, 2))
                    nc.scalar.copy(xs_t[:, buf], ps_g[:]).then_inc(s_xs, 1)

                def gates(h, buf):
                    act.wait_ge(s_gates, done(layer, h, buf))
                    act.wait_ge(s_msg, done(layer, h, buf, 2))
                    steps.then(nc.scalar.activation(gv[:, buf, 1], ps_gv[:, buf, 1], ACT.Abs))
                    act.wait_ge(s_fold, done(layer, h, buf))
                    both = gv[:, buf].rearrange("p k c -> p (k c)")
                    steps.then(nc.scalar.activation(both, both, ACT.Exp, scale=-1.0))
                    steps.then(nc.scalar.activation(both, both, ACT.Ln, bias=1.0))
                    nc.scalar.activation(both[:, 0:COLS], both[:, 0:COLS], ACT.Exp, scale=-1.0).then_inc(s_lns, 1)

                def copy_sums(h, buf):
                    act.wait_ge(s_turned, done(layer, h, buf))
                    act.wait_ge(s_stored[buf], stored(layer, h, 1))
                    nc.scalar.copy(sums[:, buf], ps_out[:]).then_inc(s_sums, 1)

                nc.scalar.preload_act_table_set("natural_log_exp_and_others")
                pipeline(act, (copy_rows, 0), (gates, 1), (copy_sums, 2), steps=steps, per=6)

                if layer == 0:
                    for a in range(ACCS):
                        rows_a = acc_d[a].rearrange("(p r) f -> p (r f)", p=P)
                        for k in range(2):
                            if a or k:
                                act.wait_ge(s_tables, 16 * (2 * a + k))
                            act.dma_start(rows_a[:, k * ZW:(k + 1) * ZW], zeros[:]).then_inc(s_tables, 16)
                for half in range(2):
                    act.wait_ge(s_centred, 2 * layer + half + 1)
                    nc.scalar.activation(squares[:, halves[half]], H[:, halves[half]],
                                         ACT.Square).then_inc(s_squared, 1)
                act.wait_ge(s_var, layer + 1)
                nc.scalar.activation(stat[:, 4], stat[:, 4], ACT.Sqrt).then_inc(s_std, 1)
                if layer == 0:
                    with act.Fori(0, CP) as i:
                        for buf in range(2):
                            wait(s_stage, cdone(1, i, buf))
                            nc.scalar.copy(H[:, chunk(i, buf)], stage[:, buf]).then_inc(s_hcopy, 1)
                    continue
                with act.Fori(0, CP) as i:
                    for buf in range(2):
                        act.wait_ge(s_lnv, cdone(0, i, buf))
                        nc.scalar.activation(small[:, buf, 2], small[:, buf, 2], ACT.Sqrt).then_inc(s_lnr, 1)
                        wait(s_z, cdone(0, i, buf))
                        nc.scalar.copy(H[:, chunk(i, buf)], z[:, buf]).then_inc(s_hcopy, 1)
                        act.wait_ge(s_zt, cdone(0, i, buf))
                        act.wait_ge(s_wh, cdone(0, i, buf, 2))
                        for k, n in ((0, TILES * P), (1, (CH - TILES) * P)):
                            c = nc.scalar.copy(x2_t[0:D, buf, k * COLS:k * COLS + n], ps_gv[0:D, 0, k, 0:n])
                        c.then_inc(s_ztc, 1)
                        act.wait_ge(s_wh, cdone(0, i, buf))
                        act.wait_ge(s_scat, scattered(2, i, buf - 2))
                        act.wait_ge(s_table[buf], tabled(1, i, 1))
                        nc.scalar.copy(stage[:, buf], ps_out[:, 0:CW]).then_inc(s_stage, 1)
                        nc.scalar.mul(X[:, chunk(i, buf)], ps_out[:, 0:CW], coef[:, 10:11]).then_inc(s_whc, 1)

            def dst_rows(h, buf):
                act.wait_ge(s_wt, done(0, h, buf))
                act.wait_ge(s_wm, done(0, h, buf, 2))
                nc.scalar.copy(wc[:, buf], ps_g[:]).then_inc(s_wc, 1)
                act.wait_ge(s_n2, done(0, h, buf, 1))
                nc.scalar.activation(sq[:, 0:SLOTS * D], ps_g[:], ACT.Square)

            def copy_put(h, buf):
                act.wait_ge(s_comb, done(0, h, buf))
                put_before(act, h, buf)
                nc.scalar.copy(put[:, buf], ps_out[:]).then_inc(s_put, 1)

            def src_squares(h, buf):
                act.wait_ge(s_gath[buf], gathered(2, h, buf))
                nc.scalar.activation(sq[:, SLOTS * D:], G[:, buf], ACT.Square).then_inc(s_sq, 1)
                act.wait_ge(s_n2, done(0, h, buf))
                nc.scalar.activation(dots[:, 3], dots[:, 3], ACT.Sqrt).then_inc(s_nn, 1)

            pipeline(act, (dst_rows, 0), (copy_put, 1), (src_squares, 0))

            with act.Fori(0, CP) as i:
                for buf in range(2):
                    act.wait_ge(s_lnv, cdone(1, i, buf))
                    nc.scalar.activation(small[:, buf, 2], small[:, buf, 2], ACT.Sqrt).then_inc(s_lnr, 1)

        @block.vector
        def _(dve):
            v = nc.vector
            steps = Steps(dve, s_dve)
            then = steps.then
            v.memset(zeros[:], 0.0).then_inc(s_zeros, 1)
            for s in by_two:
                dve.sem_inc(s, 2)
            for pair in by_sp:
                for s in pair:
                    dve.sem_inc(s, 16)
            for t in (w_dst, w_src):
                v.memset(t[:], 0.0)
            v.memset(w_attr[:], 0.0).then_inc(s_tiles, 1)
            v.memset(ones[:], 1.0)
            v.memset(attr[2 * DA:2 * DA + 1], 1.0)
            v.memset(x2_t[D:D + 1], 1.0)
            steps.begin()
            then(v.memset(xd_t[:, 1, COLS - 1:COLS], 0.0))
            dve.wait_ge(s_search, 48)
            v.tensor_tensor(same_all[:], dst_now, dst_was, ALU.is_equal).then_inc(s_same_set, 1)
            then(v.tensor_copy(last_f, last_i))
            dve.wait_ge(s_pool, 7)
            then(v.tensor_copy(node_id[:], node_id_i[:]))
            then(v.tensor_copy(drop[:], drop_i[:]))
            steps.end()


            def stage_idx(rnd, h, buf):
                if rnd or not at_start(h):
                    dve.wait_ge(s_scat, scattered(rnd, h, buf - 2))
                v.tensor_scalar(put_nodes[:, buf], first_idx[:, ccols(h, buf)], 0.0, None,
                                ALU.add).then_inc(s_pnodes, 1)

            def find_blocks(at, buf, n):
                then(v.tensor_scalar(search[:, buf, 0, 0:n], node_id[:, at], 0.0, None, ALU.add))
                for c in range(n):
                    then(v.tensor_scalar(junk, last_f, search[:, buf, 0, c:c + 1], 0.0, ALU.is_lt, ALU.add,
                                         accum_out=search[:, buf, 1, c:c + 1]))
                then(v.tensor_scalar(search[:, buf, 2, 0:n], search[:, buf, 1, 0:n], float(SEARCH - 1), None, ALU.min))
                return v.tensor_scalar(block_idx[:, buf, 0:n], search[:, buf, 2, 0:n], 0.0, None, ALU.add)

            def find_edges(at, buf, n):
                for c in range(n):
                    then(v.tensor_scalar(junk, block_rows[:, buf, c], search[:, buf, 0, c:c + 1], 0.0, ALU.is_lt,
                                         ALU.add, accum_out=search[:, buf, 1, c:c + 1]))
                then(v.scalar_tensor_tensor(first[:, at], search[:, buf, 2, 0:n], float(SEARCH),
                                            search[:, buf, 1, 0:n], ALU.mult, ALU.add))

            def find_block(h, buf):
                find_blocks(ccols(h, buf), buf, CH).then_inc(s_bidx, 1)

            def find_edge(h, buf):
                dve.wait_ge(s_rows[buf], h * (16 * CH) + 16 * CH)
                find_edges(ccols(h, buf), buf, CH)

            def stage_x(h, buf):
                now = ccols(h, buf)
                f, e, ok, r, idx_now = (w[:, at] for w, at in (
                    (first, now), (first, ds(h * (2 * CH) + buf * CH + 1, CH)), (valid, now), (row, now),
                    (first_idx, now)))
                then(v.tensor_tensor(ok, e, f, ALU.is_gt))
                then(v.scalar_tensor_tensor(ok, node_id[:, now], float(N), ok, ALU.is_lt, ALU.mult))
                then(v.tensor_scalar(r, f, float(HALF), float(EP - 1), ALU.is_ge, ALU.mult))
                then(v.scalar_tensor_tensor(r, f, 2.0, r, ALU.mult, ALU.subtract))
                then(v.scalar_tensor_tensor(idx_now, r, drop[:, 0:1], ok, ALU.subtract, ALU.mult))
                then(v.tensor_scalar(idx_now, idx_now, drop[:, 0:1], None, ALU.add))
                stage_idx(0, h, buf)
                v.tensor_scalar(stage[:, buf], X[:, chunk(h, buf)], 1.0, None, ALU.mult).then_inc(s_stage, 1)

            steps.begin()
            end = slice(NT, NT + 1)
            find_blocks(end, 1, 1).then_inc(s_end_idx, 1)
            dve.wait_ge(s_end_rows, 16)
            find_edges(end, 1, 1)
            steps.end()
            dve.wait_ge(s_nodes, 32)
            pipeline(dve, (find_block, 0), (find_edge, 1), (stage_x, 2), steps=steps, per=2 * (CH + 2 + CH + 1 + 6),
                     pairs=CP, peel=1)

            steps.begin()
            f, e = first[:, 0:NT], first[:, 1:NT + 1]
            then(v.tensor_scalar(row, e, float(HALF), float(EP - 1), ALU.is_gt, ALU.mult))
            then(v.scalar_tensor_tensor(row, e, 2.0, row, ALU.mult, ALU.subtract))
            then(v.scalar_tensor_tensor(last_idx[:], row, float(EP + 2), valid, ALU.subtract, ALU.mult))
            then(v.tensor_scalar(last_idx[:], last_idx[:], float(EP), None, ALU.add))
            then(v.tensor_scalar(seam[:], f, float(HALF), None, ALU.is_lt))
            then(v.scalar_tensor_tensor(seam[:], e, float(HALF), seam[:], ALU.is_gt, ALU.mult))

            dve.wait_ge(s_edges, 16 * 8)
            then(v.tensor_scalar(deg, deg, coef_in[:, 0:1], coef_in[:, 1:2], ALU.mult, ALU.add))
            then(v.scalar_tensor_tensor(deg_tmp, deg, -1.0, deg, ALU.mult, ALU.min))
            then(v.tensor_reduce(coef[:, 4:5], coef_in[:, 2:5], AX.X, ALU.max))
            then(v.tensor_scalar(coef[:, 0:3], coef_in[:, 2:5], coef[:, 4:5], None, ALU.subtract))
            v.scalar_tensor_tensor(coef[:, 3:4], coef_in[:, 5:6], -1.0, coef_in[:, 5:6], ALU.mult,
                                   ALU.min).then_inc(s_deg, 1)
            steps.end()

            steps.begin()
            dve.wait_ge(s_dega, 1)
            then(v.scalar_tensor_tensor(deg, deg, 0.0, deg_tmp, ALU.max, ALU.add))
            then(v.tensor_tensor(deg_tmp, src_i, dst_i, ALU.not_equal))
            then(v.tensor_tensor(weight[:], weight[:], deg, ALU.mult))
            then(v.tensor_tensor(weight[:], weight[:], deg_tmp, ALU.mult))
            then(v.scalar_tensor_tensor(coef[:, 5:6], coef_in[:, 5:6], 0.0, coef[:, 3:4], ALU.max, ALU.add))
            then(v.tensor_reduce(coef[:, 6:7], coef[:, 0:3], AX.X, ALU.add))
            then(v.reciprocal(coef[:, 7:8], coef[:, 6:7]))
            then(v.tensor_tensor(coef[:, 7:8], coef[:, 7:8], coef[:, 5:6], ALU.mult))
            then(v.tensor_scalar(coef[:, 8:11], coef[:, 0:3], coef[:, 7:8], None, ALU.mult))
            then(v.memset(sum_t[:, 1, COLS - 1:COLS], 0.0))
            dve.sem_inc(s_setup, 1)
            steps.end()

            def carry_dst(layer, h, buf):
                dve.wait_ge(s_injt, done(layer, h, buf))
                dve.wait_ge(s_load[buf], loaded(layer, h))
                if layer < 2:
                    dve.wait_ge(s_gates, done(layer, h, buf, 2))
                else:
                    dve.wait_ge(s_wt, done(0, h, buf, 2))
                dve.wait_ge(s_scan, done(layer, h, buf, 1))
                v.tensor_tensor_scan(xd_t[:, buf], same[:, buf], ps_inj[:], xd_t[:, 1 - buf, COLS - 1:COLS],
                                     ALU.mult, ALU.add).then_inc(s_scan, 1)

            def layer_norm(t, rnd, h, buf):
                m = small[:, buf]
                then(v.tensor_reduce(m[:, 0], by_node(t), AX.X, ALU.add))
                then(v.tensor_scalar(m[:, 1], m[:, 0], -1.0 / D, None, ALU.mult))
                then(v.tensor_tensor(t, by_node(t), along(m[:, 1], D), ALU.add))
                then(v.tensor_tensor(tmp[:], t, t, ALU.mult))
                then(v.tensor_reduce(m[:, 3], by_node(tmp[:]), AX.X, ALU.add))
                v.tensor_scalar(m[:, 2], m[:, 3], 1.0 / D, EPS, ALU.mult, ALU.add).then_inc(s_lnv, 1)
                dve.wait_ge(s_lnr, cdone(rnd, h, buf))
                then(v.reciprocal(m[:, 4], m[:, 2]))
                return v.tensor_tensor(t, by_node(t), along(m[:, 4], D), ALU.mult)

            for layer in range(2):
                def carry(h, buf):
                    carry_dst(layer, h, buf)

                def fold(h, buf):
                    dve.wait_ge(s_gates, done(layer, h, buf))
                    v.tensor_scalar(gv[:, buf, 0], ps_gv[:, buf, 0], GATE_MIN, None, ALU.max).then_inc(s_fold, 1)

                def messages(h, buf):
                    dve.wait_ge(s_lns, done(layer, h, buf))
                    v.scalar_tensor_tensor(soft, ps_gv[:, buf, 1], 0.0, gv[:, buf, 1], ALU.max,
                                           ALU.add).then_inc(s_soft, 1)
                    dve.wait_ge(s_soft, done(layer, h, buf))
                    v.tensor_tensor(msg, gv[:, buf, 0], soft, ALU.mult).then_inc(s_msg, 1)
                    dve.wait_ge(s_msg, done(layer, h, buf))
                    dve.wait_ge(s_turned, done(layer, h, buf, 2))
                    dve.wait_ge(s_sumt, done(layer, h, buf, 1))
                    dve.wait_ge(s_same_sum[buf], loaded_one(32, layer, h))
                    v.tensor_tensor_scan(sum_t[:, buf], same_sum[:, buf], msg, sum_t[:, 1 - buf, COLS - 1:COLS],
                                         ALU.mult, ALU.add).then_inc(s_sumt, 1)

                pipeline(dve, (carry, 0), (messages, 2), (fold, 1))

                def stage_get(h, buf):
                    v.tensor_scalar(get_nodes[:, buf], last_idx[:, ccols(h, buf)], 0.0, None,
                                    ALU.add).then_inc(s_gnodes, 1)

                def add_sums(h, buf):
                    hc = H[:, chunk(h, buf)]
                    then(v.tensor_tensor(by_node(tmp[:]), along(seam[:, ccols(h, buf)], D),
                                         across(seam_row[:], CH), ALU.mult))
                    dve.wait_ge(s_agg[buf], h * (16 * CH) + 16 * CH * (layer * CP + 1))
                    then(v.tensor_tensor(hc, hc, agg[:, buf], ALU.add))
                    then(v.tensor_tensor(hc, hc, tmp[:], ALU.add))
                    then(v.tensor_tensor(total[:], total[:], hc, ALU.add))

                dve.wait_ge(s_seam, 16 * (layer + 1))
                if layer:
                    dve.wait_ge(s_pads, 16)
                steps.begin()
                then(v.memset(total[:], 0.0))
                stage_get(0, 0)
                stage_get(0, 1)
                steps.end()
                with dve.Fori(0, CP - 1) as i:
                    steps.begin(i, 8)
                    for buf in range(2):
                        add_sums(i, buf)
                        stage_get(i + 1, buf)
                steps.end(CP - 1, 8)
                steps.begin()
                for buf in range(2):
                    add_sums(CP - 1, buf)
                dve.sem_inc(s_part, 1)
                dve.wait_ge(s_tot, 2 * layer + 1)
                then(v.tensor_reduce(stat[:, 0], ps_out[:, 0:CW].rearrange("p (c f) -> p f c", f=D), AX.X, ALU.add))
                then(v.scalar_tensor_tensor(stat[:, 1], stat[:, 0], -1.0 / N, norm_w[:, layer, 2], ALU.mult, ALU.mult))
                for half in range(2):
                    hh = by_node(H[:, halves[half]])
                    v.tensor_tensor(hh, hh, across(stat[:, 1], NT // 2), ALU.add).then_inc(s_centred, 1)
                for half, to in enumerate((stat[:, 2], stat[:, 7])):
                    dve.wait_ge(s_squared, 2 * layer + half + 1)
                    then(v.tensor_reduce(to, squares[:, halves[half]].rearrange("p (t f) -> p f t", f=D), AX.X,
                                         ALU.add))
                dve.wait_ge(s_centred, 2 * layer + 2)
                v.tensor_tensor(stat[:, 2], stat[:, 2], stat[:, 7], ALU.add).then_inc(s_part, 1)
                dve.wait_ge(s_tot, 2 * layer + 2)
                then(v.tensor_tensor(stat[:, 3], stat[:, 1], stat[:, 1], ALU.mult))
                then(v.scalar_tensor_tensor(stat[:, 3], stat[:, 3], float(N - NP), ps_out[:, 0:D], ALU.mult, ALU.add))
                v.tensor_scalar(stat[:, 4], stat[:, 3], 1.0 / N, EPS, ALU.mult, ALU.add).then_inc(s_var, 1)
                dve.wait_ge(s_std, layer + 1)
                then(v.reciprocal(stat[:, 5], stat[:, 4]))
                then(v.tensor_tensor(stat[:, 6], stat[:, 5], norm_w[:, layer, 0], ALU.mult))
                steps.end()

                with dve.Fori(0, CP) as i:
                    steps.begin(i, 4 if layer == 0 else 20)
                    for buf in range(2):
                        hc = H[:, chunk(i, buf)]
                        stage_idx(layer + 1, i, buf)
                        then(v.tensor_tensor(by_node(tmp[:]), by_node(hc), across(stat[:, 6], CH), ALU.mult))
                        then(v.tensor_tensor(by_node(tmp[:]), by_node(tmp[:]), across(norm_w[:, layer, 1], CH), ALU.add))
                        if layer == 0:
                            dve.wait_ge(s_table[buf], tabled(0, i, 1))
                            dve.wait_ge(s_hcopy, cdone(0, i, buf, 2))
                            v.scalar_tensor_tensor(stage[:, buf], tmp[:], SLOPE, tmp[:], ALU.mult,
                                                   ALU.max).then_inc(s_stage, 1)
                            dve.wait_ge(s_stage, cdone(1, i, buf))
                            continue
                        dve.wait_ge(s_zt, cdone(0, i, buf, 2))
                        dve.wait_ge(s_hcopy, cdone(1, i, buf, 2))
                        then(v.scalar_tensor_tensor(z[:, buf], tmp[:], SLOPE, tmp[:], ALU.mult, ALU.max))
                        then(v.tensor_tensor(z[:, buf], z[:, buf], X[:, chunk(i, buf)], ALU.add))
                        layer_norm(z[:, buf], 0, i, buf).then_inc(s_z, 1)
                steps.end(CP, 4 if layer == 0 else 20)

            dve.wait_ge(s_whc, cdone(0, CP - 1, 1))
            v.tensor_tensor(H[:], H[:], X[:], ALU.add).then_inc(s_base, 1)
            dve.wait_ge(s_base, 1)

            drop_node = drop[:, 1:2]
            def last_layer(i):
                for buf in range(2):
                    carry_dst(2, i, buf)
                    dve.wait_ge(s_idx[buf], i * 16 + 16 * (2 * PAIRS + 1))
                    dve.wait_ge(s_srcb, done(0, i, buf, 2))
                    v.tensor_copy(src_f[:, buf], idx[:, buf]).then_inc(s_srcf, 1)
                    dve.wait_ge(s_srcf, done(0, i, buf))
                    dve.wait_ge(s_srcb, done(0, i, buf))
                    dve.wait_ge(s_comb, done(0, i, buf, 2))
                    equal_now = equal[:, buf].rearrange("p (k e) -> p k e", e=P)
                    v.tensor_tensor(equal_now, ps_gv[:, buf].rearrange("p k (t e) -> p (k t) e", e=P),
                                    along(src_f[:, buf], P), ALU.is_equal).then_inc(s_equal, 1)
                    dve.wait_ge(s_equal, done(0, i, buf))
                    then(v.tensor_tensor(earlier, equal_now, across(before[:], SLOTS), ALU.mult))
                    then(v.tensor_reduce(dots[:, 6], earlier, AX.X, ALU.add))
                    then(v.tensor_scalar(dots[:, 7], src_f[:, buf], drop_node, None, ALU.subtract))
                    then(v.scalar_tensor_tensor(dots[:, 8], dots[:, 6], 0.0, dots[:, 7], ALU.is_equal, ALU.mult))
                    put_before(dve, i, buf)
                    v.tensor_scalar(put_idx[:, buf], dots[:, 8], drop_node, None, ALU.add).then_inc(s_pidx, 1)
                    dve.wait_ge(s_wc, done(0, i, buf))
                    dve.wait_ge(s_gath[buf], gathered(2, i, buf))
                    then(v.tensor_tensor(prod, G[:, buf], wc[:, buf], ALU.mult))
                    then(v.tensor_reduce(dots[:, 0], by_node(prod), AX.X, ALU.add))
                    dve.wait_ge(s_sq, done(0, i, buf))
                    v.tensor_reduce(dots[:, 1:3].rearrange("p a k -> p (a k)"), by_node(sq), AX.X, ALU.add).then_inc(s_used, 1)
                    dve.wait_ge(s_used, done(0, i, buf))
                    then(v.tensor_tensor(dots[:, 4], dots[:, 1], dots[:, 2], ALU.mult))
                    v.tensor_scalar(dots[:, 3], dots[:, 4], SIM_EPS * SIM_EPS, None, ALU.max).then_inc(s_n2, 1)
                    dve.wait_ge(s_nn, done(0, i, buf))
                    then(v.reciprocal(dots[:, 5], dots[:, 3]))
                    then(v.tensor_tensor(dots[:, 9], dots[:, 0], dots[:, 5], ALU.mult))
                    then(v.tensor_scalar(dots[:, 10], dots[:, 9], 0.0, coef[:, 8:9], ALU.max, ALU.mult))
                    then(v.tensor_scalar(dots[:, 11], dots[:, 9], 0.0, coef[:, 9:10], ALU.min, ALU.mult))
                    then(v.tensor_tensor(dots[:, 10], dots[:, 10], dots[:, 11], ALU.add))
                    then(v.tensor_tensor(dots[:, 9], dots[:, 10], weight[:, ds(i * (2 * SLOTS) + buf * SLOTS, SLOTS)],
                                         ALU.mult))
                    v.tensor_tensor(w_msg[:, buf], by_node(wc[:, buf]), along(dots[:, 9], D), ALU.mult).then_inc(s_wm, 1)

            steps.begin()
            last_layer(0)
            steps.end()
            with dve.Fori(1, PAIRS) as i:
                steps.begin(i - 1, 26)
                last_layer(i)
            steps.end(PAIRS - 1, 26)

            with dve.Fori(0, CP) as i:
                steps.begin(i, 18)
                for buf in range(2):
                    part = [fin[:, buf, a] for a in range(ACCS)]
                    t = z[:, buf]
                    dve.wait_ge(s_fin[buf], i * (16 * ACCS) + 16 * ACCS)
                    dve.wait_ge(s_out_st[buf], i * 16 + 16)
                    then(v.tensor_tensor(t, part[0], part[1], ALU.add))
                    then(v.tensor_tensor(t, t, part[2], ALU.add))
                    v.tensor_tensor(t, t, part[3], ALU.add).then_inc(s_fused, 1)
                    dve.wait_ge(s_fused, cdone(0, i, buf))
                    then(v.tensor_tensor(t, t, H[:, chunk(i, buf)], ALU.add))
                    layer_norm(t, 1, i, buf).then_inc(s_result, 1)
                steps.end(CP, 18)


_OUT = (N, D)


def kernel(**inputs):
    import concourse.bacc as bacc
    from concourse.bass_utils import run_bass_kernel_spmd

    a = {k: np.asarray(w) for k, w in inputs.items()}

    def edges(w, fill):
        padded = np.full((EP,) + w.shape[1:], fill, w.dtype)
        padded[:E] = w
        return padded

    def by_slot(w):
        return np.ascontiguousarray(w.reshape(2, GROUPS, P, TILES).transpose(2, 1, 3, 0).reshape(P, -1))

    x = np.zeros((NP, D), a["x"].dtype)
    x[:N] = a["x"]
    src, dst = edges(a["src"], 0), edges(a["dst"], N)
    dst_prev = np.concatenate([np.full(1, -1, dst.dtype), dst[:-1]])
    dst_prev[HALF] = -1
    attr = edges(a["edge_attr_32"], 0).reshape(2, GROUPS, COLS, DA).transpose(1, 0, 3, 2)
    arrays = {
        "x": x, "dst_rows": dst.reshape(P, EP // P), "dst_blocks": dst.reshape(SEARCH, SEARCH),
        "dst_prev": dst_prev.reshape(P, EP // P), "block_last": dst.reshape(SEARCH, SEARCH)[:, -1].reshape(1, SEARCH),
        "seam_dst": dst[HALF:HALF + 1].reshape(1, 1), "src_g": by_slot(src),
        "src_ahead": by_slot(src).reshape(P, PAIRS, 2 * SLOTS)[:, :, -1], "dst_e": by_slot(dst),
        "adj_e": by_slot(edges(a["edge_weight"], 0)), "deg_e": by_slot(edges(a["edge_weight_n2"], 0)),
        "attr_t": attr.reshape(GROUPS, 2 * DA, COLS),
    }
    for layer in (1, 2):
        for name in ("Wf", "bf", "Ws", "bs", "gw", "gb", "gm"):
            w = a[f"L0_gnn_{name}{layer}"]
            arrays[f"{name}{layer}"] = w if w.ndim == 2 else w.reshape(1, -1)
    arrays["W"] = a["L1_gnn_W"]
    for name in ("b", "deg_coeff", "coeff_param", "scale_param"):
        arrays[name] = a[f"L1_gnn_{name}"].reshape(1, -1)
    arrays = {k: np.ascontiguousarray(w) for k, w in arrays.items()}

    nc = bacc.Bacc("TRN2", target_bir_lowering=False, num_devices=1)
    ap = {k: nc.dram_tensor(f"in_{k}", w.shape, mybir.dt.from_np(w.dtype), kind="ExternalInput").ap()
          for k, w in arrays.items()}
    out = nc.dram_tensor("out", [NP, D], F32, kind="ExternalOutput").ap()
    conv = [[ap[f"{name}{layer}"] for name in ("Wf", "bf", "Ws", "bs", "gw", "gb", "gm")] for layer in (1, 2)]
    gnn(nc, ap["x"], ap["dst_rows"], ap["dst_blocks"], ap["dst_prev"], ap["block_last"], ap["seam_dst"],
        ap["src_g"], ap["src_g"], ap["src_ahead"], ap["dst_e"], ap["adj_e"], ap["deg_e"], ap["attr_t"], conv, ap["W"], ap["b"],
        ap["deg_coeff"], ap["coeff_param"], ap["scale_param"], out)
    result = run_bass_kernel_spmd(nc, [{f"in_{k}": w for k, w in arrays.items()}], core_ids=[0])
    return result.results[0]["out"][:N]
```
